# Optimizing a Trainium2 kernel written in Bass

```python
import numpy as np
import jax
import jax.numpy as jnp

def _softmax(x, axis=-1):
    return jax.nn.softmax(x, axis=axis)
def _gelu(x):
    return jax.nn.gelu(x, approximate=True)
def _silu(x):
    return jax.nn.silu(x)
def _sigmoid(x):
    return jax.nn.sigmoid(x)
def _layernorm(x, axis=-1, eps=1e-5):
    m = jnp.mean(x, axis=axis, keepdims=True)
    v = jnp.var(x, axis=axis, keepdims=True)
    return (x - m) / jnp.sqrt(v + eps)
def _scatter_add(tgt, idx, src, axis=0):
    return tgt.at[idx].add(src)
def _segment_sum(src, seg, n):
    return jax.ops.segment_sum(src, seg, n)

kernel_name = 'mk_conv_seq_d1_conv_nhwc512_91566b'

def setup_inputs(seed: int = 0):
    np.random.seed(seed)
    _w = jnp.asarray
    def _rec_inputs():
        import jax
        import jax.numpy as jnp
        _gk = jax.random.key(seed)
        x = -0.0005847 + 1 * jax.random.normal(jax.random.fold_in(_gk, 1), (8, 30, 30, 512), jnp.float32)
        return x
    x = _rec_inputs()
    def _L0_conv_setup():
        import jax, jax.numpy as jnp
        import numpy as np
        B, GH, GW, D = (8, 30, 30, 512)
        NH, FF = (8, 2048)
        DK = D // NH
        LN_EPS = 1e-05

        def _spatial_indices(H, W):
            hs = np.arange(H * W) // W
            ws = np.arange(H * W) % W
            dh = hs[None, :] - hs[:, None]
            dw = ws[None, :] - ws[:, None]
            dist = np.sqrt(dh.astype(np.float64) ** 2 + dw.astype(np.float64) ** 2)
            dist_idx = np.minimum(dist.astype(np.int64), 59)
            angle = np.arctan2(dh.astype(np.float64), dw.astype(np.float64)) + np.pi
            dir_idx = (angle / (2.0 * np.pi) * 16.0).astype(np.int64) % 16
            dir_idx = np.where((dh == 0) & (dw == 0), 0, dir_idx)
            return (jnp.asarray(dist_idx), jnp.asarray(dir_idx))

        def _layer_norm(x, g, b):
            m = jnp.mean(x, axis=-1, keepdims=True)
            v = jnp.mean(jnp.square(x - m), axis=-1, keepdims=True)
            return (x - m) * jax.lax.rsqrt(v + LN_EPS) * g + b
        key = jax.random.key(seed)
        ks = jax.random.split(key, 16)
        s = 0.02
        return {'x': jax.random.normal(ks[0], (B, GH, GW, D), dtype=jnp.float32), 'w_q': jax.random.normal(ks[1], (D, D), dtype=jnp.float32) * s, 'b_q': jnp.zeros((D,), jnp.float32), 'w_k': jax.random.normal(ks[2], (D, D), dtype=jnp.float32) * s, 'b_k': jnp.zeros((D,), jnp.float32), 'w_v': jax.random.normal(ks[3], (D, D), dtype=jnp.float32) * s, 'b_v': jnp.zeros((D,), jnp.float32), 'w_o': jax.random.normal(ks[4], (D, D), dtype=jnp.float32) * s, 'b_o': jnp.zeros((D,), jnp.float32), 'dist_bias': jax.random.normal(ks[5], (60, NH), dtype=jnp.float32) * s, 'dir_bias': jax.random.normal(ks[6], (16, NH), dtype=jnp.float32) * s, 'ln1_g': jnp.ones((D,), jnp.float32), 'ln1_b': jnp.zeros((D,), jnp.float32), 'w1': jax.random.normal(ks[7], (D, FF), dtype=jnp.float32) * s, 'b1': jnp.zeros((FF,), jnp.float32), 'w2': jax.random.normal(ks[8], (FF, D), dtype=jnp.float32) * s, 'b2': jnp.zeros((D,), jnp.float32), 'ln2_g': jnp.ones((D,), jnp.float32), 'ln2_b': jnp.zeros((D,), jnp.float32)}
    _L0_conv_all = _L0_conv_setup()
    _L0_conv_in = {k: v for k, v in _L0_conv_all.items() if k in ('w_q', 'b_q', 'w_k', 'b_k', 'w_v', 'b_v', 'w_o', 'b_o', 'dist_bias', 'dir_bias', 'ln1_g', 'ln1_b', 'w1', 'b1', 'w2', 'b2', 'ln2_g', 'ln2_b', )}
    del _L0_conv_all

    return {
        "x": x,
        "L0_conv_w_q": _L0_conv_in["w_q"],
        "L0_conv_b_q": _L0_conv_in["b_q"],
        "L0_conv_w_k": _L0_conv_in["w_k"],
        "L0_conv_b_k": _L0_conv_in["b_k"],
        "L0_conv_w_v": _L0_conv_in["w_v"],
        "L0_conv_b_v": _L0_conv_in["b_v"],
        "L0_conv_w_o": _L0_conv_in["w_o"],
        "L0_conv_b_o": _L0_conv_in["b_o"],
        "L0_conv_dist_bias": _L0_conv_in["dist_bias"],
        "L0_conv_dir_bias": _L0_conv_in["dir_bias"],
        "L0_conv_ln1_g": _L0_conv_in["ln1_g"],
        "L0_conv_ln1_b": _L0_conv_in["ln1_b"],
        "L0_conv_w1": _L0_conv_in["w1"],
        "L0_conv_b1": _L0_conv_in["b1"],
        "L0_conv_w2": _L0_conv_in["w2"],
        "L0_conv_b2": _L0_conv_in["b2"],
        "L0_conv_ln2_g": _L0_conv_in["ln2_g"],
        "L0_conv_ln2_b": _L0_conv_in["ln2_b"],
    }

def reference(x, L0_conv_w_q, L0_conv_b_q, L0_conv_w_k, L0_conv_b_k, L0_conv_w_v, L0_conv_b_v, L0_conv_w_o, L0_conv_b_o, L0_conv_dist_bias, L0_conv_dir_bias, L0_conv_ln1_g, L0_conv_ln1_b, L0_conv_w1, L0_conv_b1, L0_conv_w2, L0_conv_b2, L0_conv_ln2_g, L0_conv_ln2_b):
    import jax
    import jax.numpy as jnp
    def _L0_conv_ref(x, w_q, b_q, w_k, b_k, w_v, b_v, w_o, b_o, dist_bias, dir_bias, ln1_g, ln1_b, w1, b1, w2, b2, ln2_g, ln2_b):
        import jax, jax.numpy as jnp
        import numpy as np
        B, GH, GW, D = (8, 30, 30, 512)
        NH, FF = (8, 2048)
        DK = D // NH
        LN_EPS = 1e-05

        def _spatial_indices(H, W):
            hs = np.arange(H * W) // W
            ws = np.arange(H * W) % W
            dh = hs[None, :] - hs[:, None]
            dw = ws[None, :] - ws[:, None]
            dist = np.sqrt(dh.astype(np.float64) ** 2 + dw.astype(np.float64) ** 2)
            dist_idx = np.minimum(dist.astype(np.int64), 59)
            angle = np.arctan2(dh.astype(np.float64), dw.astype(np.float64)) + np.pi
            dir_idx = (angle / (2.0 * np.pi) * 16.0).astype(np.int64) % 16
            dir_idx = np.where((dh == 0) & (dw == 0), 0, dir_idx)
            return (jnp.asarray(dist_idx), jnp.asarray(dir_idx))

        def _layer_norm(x, g, b):
            m = jnp.mean(x, axis=-1, keepdims=True)
            v = jnp.mean(jnp.square(x - m), axis=-1, keepdims=True)
            return (x - m) * jax.lax.rsqrt(v + LN_EPS) * g + b
        Bsz, H, W, d = x.shape
        S = H * W
        x_seq = x.reshape(Bsz, S, d)

        def heads(y):
            return y.reshape(Bsz, S, NH, DK).transpose(0, 2, 1, 3)
        q = heads(x_seq @ w_q + b_q)
        k = heads(x_seq @ w_k + b_k)
        v = heads(x_seq @ w_v + b_v)
        dist_idx, dir_idx = _spatial_indices(H, W)
        bias = (dist_bias[dist_idx] + dir_bias[dir_idx]).transpose(2, 0, 1)
        scores = jnp.einsum('bhid,bhjd->bhij', q, k) / jnp.sqrt(jnp.float32(DK))
        attn = jax.nn.softmax(scores + bias[None], axis=-1)
        ctx = jnp.einsum('bhij,bhjd->bhid', attn, v)
        ctx = ctx.transpose(0, 2, 1, 3).reshape(Bsz, S, d)
        attn_out = _layer_norm(ctx @ w_o + b_o + x_seq, ln1_g, ln1_b)
        h = jax.nn.gelu(attn_out @ w1 + b1, approximate=False)
        ff = h @ w2 + b2
        out = _layer_norm(ff + attn_out, ln2_g, ln2_b)
        return out.reshape(Bsz, H, W, d)

    def _gn(v, G=32, eps=1e-5):
        B_, H_, W_, C_ = v.shape
        g = v.reshape(B_, H_, W_, G, C_ // G)
        m = jnp.mean(g, axis=(1, 2, 4), keepdims=True)
        s = jnp.var(g, axis=(1, 2, 4), keepdims=True)
        return ((g - m) / jnp.sqrt(s + eps)).reshape(v.shape)

    def _ln_c(v, eps=1e-6):
        m = jnp.mean(v, axis=-1, keepdims=True)
        s = jnp.var(v, axis=-1, keepdims=True)
        return (v - m) / jnp.sqrt(s + eps)

    def _ln_t(v, eps=1e-5):
        m = jnp.mean(v, axis=-1, keepdims=True)
        s = jnp.var(v, axis=-1, keepdims=True)
        return (v - m) / jnp.sqrt(s + eps)

    def _to_tokens(v):
        B_, H_, W_, C_ = v.shape
        return v.reshape(B_, H_ * W_, C_)
    def _from_tokens(t, like):
        return t.reshape(like.shape)

    x = _L0_conv_ref(x, L0_conv_w_q, L0_conv_b_q, L0_conv_w_k, L0_conv_b_k, L0_conv_w_v, L0_conv_b_v, L0_conv_w_o, L0_conv_b_o, L0_conv_dist_bias, L0_conv_dir_bias, L0_conv_ln1_g, L0_conv_ln1_b, L0_conv_w1, L0_conv_b1, L0_conv_w2, L0_conv_b2, L0_conv_ln2_g, L0_conv_ln2_b)
    return x


_drawn_inputs = setup_inputs


def setup_inputs(seed=0):
    import zlib

    import numpy as np

    out = dict(_drawn_inputs(seed))
    spreads = {'L0_conv_b_q': (0.0, 0.8),
     'L0_conv_b_k': (0.0, 2.0),
     'L0_conv_b_v': (0.0, 0.329),
     'L0_conv_b_o': (0.0, 0.1),
     'L0_conv_ln1_g': (1.0, 0.2),
     'L0_conv_ln1_b': (0.0, 0.1),
     'L0_conv_b1': (0.0, 0.1),
     'L0_conv_b2': (0.0, 0.1),
     'L0_conv_ln2_g': (1.0, 0.2),
     'L0_conv_ln2_b': (0.0, 0.1)}
    factors = {'L0_conv_w_q': 8.0,
     'L0_conv_w_k': 8.0,
     'L0_conv_w_v': 7.861,
     'L0_conv_dist_bias': 8.0,
     'L0_conv_dir_bias': 8.0}
    for name, (base, spread) in spreads.items():
        noise = np.random.default_rng([zlib.crc32(name.encode()), seed]).standard_normal(out[name].shape)
        drawn = base * np.exp(spread * noise) if base else spread * noise
        out[name] = jnp.asarray(drawn.astype(out[name].dtype))
    for name, factor in factors.items():
        out[name] = (out[name] * factor).astype(out[name].dtype)
    return out
```

```python
from contextlib import ExitStack

import concourse.bass as bass
from concourse import mybir

F32 = mybir.dt.float32
F32R = mybir.dt.float32r
I32 = mybir.dt.int32
ALU = mybir.AluOpType
ACT = mybir.ActivationFunctionType

P = 128
IMAGES, GRID, D = 8, 30, 512
S = GRID * GRID
NH = 8
DK = D // NH
FF = 2048
KC = D // P
PAIRS = NH // 2
FC = FF // P
LN_EPS = 1e-5
DISTS, DIRS = 60, 16

ROWS = 4
TILE = ROWS * GRID
TILES = -(-GRID // ROWS)
LAST = S - (TILES - 1) * TILE
SPAD = TILES * TILE
HALF = S // 2
SHIFTS = GRID + ROWS * (TILES - 1) + 2
UROWS, UCOLS = SHIFTS + ROWS - 1, 2 * GRID - 1
WINDOW = SHIFTS * GRID
SCALE = DK ** -0.5


def tile_rows(t):
    return TILE if t < TILES - 1 else LAST


def prepare_tables(nc, dram, bias, wv_hi, wv_lo):
    with ExitStack() as ctx:
        def sb(name, shape, dt=F32):
            return ctx.enter_context(nc.sbuf_tensor(name, shape, dt))

        def sem(name):
            return ctx.enter_context(nc.semaphore(name))

        CH = 413
        NCH = UROWS * UCOLS // CH
        assert NCH * CH == UROWS * UCOLS
        table = sb("table", [DISTS + DIRS, NH])
        onehot = sb("onehot", [DISTS + DIRS, UROWS * UCOLS])
        u_sb = sb("u_sb", [NH, UROWS * UCOLS])
        raw = sb("raw", [P, 3, KC, D])
        qk_split = sb("qk_split", [P, PAIRS, 2, 2, KC, P], F32R)
        u_ps = ctx.enter_context(nc.psum_tensor("u_ps", [P, 4, 512], F32))

        table_landed = sem("table_landed")
        raw_landed = sem("raw_landed")
        u_ready = sem("u_ready")
        u_copied = sem("u_copied")
        skew_stored = sem("skew_stored")
        bias_landed = sem("bias_landed")
        w_hi_done = sem("w_hi_done")
        w_lo_done = sem("w_lo_done")
        qk_stored = sem("qk_stored")
        u_view = u_sb[:, :].rearrange("h (r c) -> h r c", c=UCOLS)

        with nc.Block() as block:
            @block.sync
            def _(sp):
                sp.dma_start(table[0:DISTS, :], dram["dist_bias"]).then_inc(table_landed, 16)
                sp.dma_start(table[DISTS:DISTS + DIRS, :], dram["dir_bias"]).then_inc(table_landed, 16)
                sp.dma_start(onehot[:, :], dram["displacement_onehot"]).then_inc(table_landed, 16)
                for i, name in enumerate(("w_q", "w_k", "w_v")):
                    sp.dma_start(raw[:, i], dram[name].rearrange("(k p) n -> p k n", p=P)).then_inc(raw_landed, 16)
                sp.wait_ge(u_copied, NCH)
                for w in range(GRID):
                    sp.dma_start(dram["skew"][:, w].rearrange("h (r c) -> h r c", c=GRID),
                                 u_view[:, :, GRID - 1 - w:2 * GRID - 1 - w]).then_inc(skew_stored, 16)
                sp.wait_ge(skew_stored, 16 * GRID)
                for a in range(ROWS):
                    o = (ROWS - 1 - a) * GRID
                    sp.dma_start(bias[a * GRID:(a + 1) * GRID, :, :],
                                 dram["skew"][:, :, o:o + WINDOW].rearrange("h w n -> w h n")).then_inc(bias_landed, 16)
                sp.wait_ge(bias_landed, 16 * ROWS)

            @block.scalar
            def _(act):
                act.wait_ge(raw_landed, 48)
                for i in range(2):
                    for c in range(PAIRS):
                        nc.scalar.activation(qk_split[:, c, i, 0], raw[:, i, :, c * P:(c + 1) * P],
                                             ACT.Copy).then_inc(w_hi_done, 1)
                nc.scalar.activation(wv_hi[:, :, :], raw[:, 2], ACT.Copy).then_inc(w_hi_done, 1)
                act.wait_ge(w_lo_done, 2 * PAIRS)
                act.dma_start(dram["qk_weights"].rearrange("c p n -> p c n"),
                              qk_split[:, :, :, :, :, :].rearrange("p c i s k n -> p c (i s k n)").bitcast(F32)).then_inc(qk_stored, 16)
                act.wait_ge(qk_stored, 16)

            @block.vector
            def _(dve):
                for j in range(NCH):
                    dve.wait_ge(u_ready, j + 1)
                    nc.vector.tensor_copy(u_sb[:, j * CH:(j + 1) * CH], u_ps[0:NH, j % 4, 0:CH]).then_inc(u_copied, 1)
                n = 0
                for i in range(2):
                    for c in range(PAIRS):
                        n += 1
                        dve.wait_ge(w_hi_done, n)
                        nc.vector.tensor_tensor(qk_split[:, c, i, 1], raw[:, i, :, c * P:(c + 1) * P],
                                                qk_split[:, c, i, 0].bitcast(F32), ALU.subtract).then_inc(w_lo_done, 1)
                dve.wait_ge(w_hi_done, n + 1)
                nc.vector.tensor_tensor(wv_lo[:, :, :], raw[:, 2], wv_hi[:, :, :].bitcast(F32),
                                        ALU.subtract).then_inc(w_lo_done, 1)

            @block.tensor
            def _(pe):
                pe.wait_ge(table_landed, 48)
                for j in range(NCH):
                    if j >= 4:
                        pe.wait_ge(u_copied, j - 3)
                    nc.tensor.matmul(u_ps[0:NH, j % 4, 0:CH], table[:, :], onehot[:, j * CH:(j + 1) * CH],
                                     start=True, stop=True).then_inc(u_ready, 1)


def attention(nc, dram, bias, wv_hi, wv_lo, images):
    with ExitStack() as ctx:
        def sb(name, shape, dt=F32):
            return ctx.enter_context(nc.sbuf_tensor(name, shape, dt))

        def ps(name):
            return ctx.enter_context(nc.psum_tensor(name, [P, 2, 512], F32))

        def sem(name):
            return ctx.enter_context(nc.semaphore(name))

        x_raw = sb("x_raw", [P, 2, S])
        x_hi = sb("x_hi", [P, KC, S], F32R)
        x_lo = sb("x_lo", [P, KC, S], F32R)
        w_qk = sb("w_qk", [P, 2, 2, KC, P], F32R)
        v = sb("v", [TILE, TILES, PAIRS, 3, DK])
        probs = sb("probs", [TILE, 3, S])
        q_f = sb("q_f", [P, 2, S])
        k_f = sb("k_f", [P, 2, S])
        q_hi2 = sb("q_hi2", [P, 2, SPAD], F32R)
        k_hilo = sb("k_hilo", [P, 2, S], F32R)
        k_hi1 = sb("k_hi1", [DK + TILES, 2, S], F32R)
        q_lom = sb("q_lom", [DK + TILES, 2, SPAD], F32R)
        ctx_sb = sb("ctx_sb", [P, 2, S])
        maxima = sb("maxima", [TILE, TILES])
        b_qk = sb("b_qk", [P, 2, PAIRS])
        bv = sb("bv", [TILE, D])
        ident = sb("ident", [TILE, TILE])
        spread = sb("spread", [TILES, TILES, TILE])
        st = [ps("st0"), ps("st1")]
        s1 = ps("s1")
        ct = ps("ct")

        x_landed = [sem("x_landed0"), sem("x_landed1")]
        x_split = sem("x_split")
        wqk_landed = sem("wqk_landed")
        small_landed = sem("small_landed")
        constants_set = sem("constants_set")
        qk_ready = sem("qk_ready")
        qk_staged = sem("qk_staged")
        head_hi = sem("head_hi")
        hi_copied = sem("hi_copied")
        lo_split = sem("lo_split")
        pool_step = sem("pool_step")
        pool_passed = sem("pool_passed")
        v_ready = sem("v_ready")
        v_staged = sem("v_staged")
        first_ready = sem("first_ready")
        first_seen = sem("first_seen")
        maxed = sem("maxed")
        turned = sem("turned")
        max_spread = sem("max_spread")
        scores_ready = sem("scores_ready")
        biased = sem("biased")
        exped = sem("exped")
        pv_done = sem("pv_done")
        ctx_copied = sem("ctx_copied")
        ctx_stored = [sem("ctx_stored0"), sem("ctx_stored1")]

        STEPS = NH * TILES
        FIRST = [[], [], [0], [1], [2], [3], [4, 5], [6, 7]]

        def halves(a):
            return a.rearrange("p (t n) -> p t n", t=2)

        def window(h, rows, top):
            stop = top - S
            return halves(bias[0:rows, h, top:(stop if stop >= 0 else None):-1])

        def stages_pair(h):
            return h // 2 + 1 if h % 2 == 0 and h // 2 + 1 < PAIRS else None

        with nc.Block() as block:
            @block.sync
            def _(sp):
                sp.dma_start(b_qk[:, 0], dram["b_q"]).then_inc(small_landed, 16)
                sp.dma_start(b_qk[:, 1], dram["b_k"]).then_inc(small_landed, 16)
                sp.dma_start(bv[:, :], dram["b_v"].to_broadcast([TILE, D])).then_inc(small_landed, 16)
                with sp.Fori(0, images) as b:
                    for k in range(KC):
                        if k >= 2:
                            sp.wait_ge(x_split, b * KC + (k - 1))
                        else:
                            sp.wait_ge(x_split, b * KC)
                        sp.dma_start(x_raw[:, k % 2, :], dram["x_t"][k * P:(k + 1) * P, bass.ds(b * S, S)])\
                          .then_inc(x_landed[k % 2], 16)
                    for c in range(PAIRS):
                        sp.wait_ge(qk_ready, b * (2 * PAIRS) + 2 * c)
                        sp.dma_start(w_qk[:, :, :, :, :].rearrange("p i s k n -> p (i s k n)").bitcast(F32),
                                     dram["qk_weights"][c]).then_inc(wqk_landed, 16)

            @block.gpsimd
            def _(pool):
                nc.gpsimd.memset(ident[:, :], 0.0).then_inc(pool_step, 1)
                nc.gpsimd.memset(spread[:, :, :], -1.0).then_inc(pool_step, 1)
                pool.wait_ge(pool_step, 2)
                nc.gpsimd.affine_select(out=ident[:, :], in_=ident[:, :], compare_op=ALU.not_equal, fill=1.0,
                                        base=0, pattern=[[-1, TILE]], channel_multiplier=1).then_inc(pool_step, 1)
                flat = spread[:, :, :].rearrange("p a n -> p (a n)")
                nc.gpsimd.affine_select(out=flat, in_=flat, compare_op=ALU.is_ge, fill=0.0, base=0,
                                        pattern=[[1, SPAD]], channel_multiplier=-TILE).then_inc(pool_step, 1)
                pool.wait_ge(pool_step, 4)
                nc.gpsimd.affine_select(out=flat, in_=flat, compare_op=ALU.is_ge, fill=0.0, base=TILE - 1,
                                        pattern=[[-1, SPAD]], channel_multiplier=TILE).then_inc(pool_step, 1)
                for t in range(TILES):
                    nc.gpsimd.memset(v[:, t, :, 1, :], 1.0).then_inc(pool_step, 1)
                pool.wait_ge(pool_step, 5 + TILES)
                nc.gpsimd.memset(q_hi2[:, :, S:SPAD].bitcast(F32), 0.0).then_inc(pool_step, 1)
                pool.wait_ge(pool_step, 6 + TILES)
                nc.gpsimd.memset(k_hi1[DK:DK + TILES, :, :].bitcast(F32), 1.0).then_inc(pool_step, 1)
                pool.wait_ge(pool_step, 7 + TILES)
                nc.gpsimd.engine_nop().then_inc(constants_set, 1)
                base = 7 + TILES
                per = KC + NH
                with pool.Fori(0, images) as b:
                    pool.wait_ge(qk_ready, b * (2 * PAIRS))
                    pool.wait_ge(v_ready, b * TILES)
                    for k in range(KC):
                        pool.wait_ge(x_landed[k % 2], (b * (KC // 2) + (k // 2 + 1)) * 16)
                        pool.sem_inc(pool_passed, 1)
                        nc.gpsimd.tensor_copy(x_hi[:, k], x_raw[:, k % 2]).then_inc(pool_step, 1)
                        pool.wait_ge(pool_step, b * per + (base + k + 1))
                        nc.gpsimd.tensor_tensor(x_lo[:, k], x_raw[:, k % 2], x_hi[:, k].bitcast(F32),
                                                ALU.subtract).then_inc(x_split, 1)
                        pool.wait_ge(x_split, b * KC + (k + 1))
                    for h in range(NH):
                        s, j, r = h % 2, (h // 2) % 2, DK * (h % 2)
                        pool.wait_ge(hi_copied, b * NH + (h + 1))
                        nc.gpsimd.tensor_tensor(q_lom[0:DK, s, 0:S], q_f[r:r + DK, j], q_hi2[r:r + DK, s, 0:S].bitcast(F32),
                                                ALU.subtract).then_inc(pool_step, 1)
                        pool.wait_ge(pool_step, b * per + (base + KC + h + 1))
                        nc.gpsimd.tensor_tensor(k_hilo[DK:P, s], k_f[r:r + DK, j], k_hilo[r:r + DK, s].bitcast(F32),
                                                ALU.subtract).then_inc(lo_split, 1)
                        pool.wait_ge(lo_split, b * NH + (h + 1))

            @block.scalar
            def _(act):
                def stage(b, i, c):
                    act.wait_ge(qk_ready, b * (2 * PAIRS) + (2 * c + i + 1))
                    act.wait_ge(lo_split, b * NH + (2 * (c - 1) if c >= 2 else 0))
                    out = halves(q_f[:, c % 2, S - 1::-1]) if i == 0 else halves(k_f[:, c % 2, :])
                    nc.scalar.activation(out, s1[:, :, 0:HALF], ACT.Identity, bias=b_qk[:, i, c:c + 1],
                                         scale=SCALE if i == 0 else 1.0).then_inc(qk_staged, 1)

                def upper(b, h, part):
                    s, j, r = h % 2, (h // 2) % 2, DK * (h % 2)
                    if part == 0:
                        act.wait_ge(qk_staged, b * (2 * PAIRS) + (2 * (h // 2) + 2))
                        act.wait_ge(scores_ready, b * STEPS + (TILES * (h - 1) if h else 0))
                        nc.scalar.activation(q_hi2[0:DK, s, 0:S], q_f[r:r + DK, j], ACT.Copy)
                        nc.scalar.activation(k_hilo[0:DK, s], k_f[r:r + DK, j], ACT.Copy).then_inc(head_hi, 1)
                    else:
                        nc.scalar.activation(q_hi2[DK:P, s, 0:S], q_f[r:r + DK, j], ACT.Copy)
                        if r:
                            nc.scalar.activation(k_hilo[DK:P, s], k_f[r:r + DK, j], ACT.Copy)
                        nc.scalar.activation(k_hi1[0:DK, s], k_f[r:r + DK, j], ACT.Copy).then_inc(hi_copied, 1)

                def exponentials(b, h, t):
                    act.wait_ge(biased, b * STEPS + (TILES * h + t + 1))
                    a = probs[0:tile_rows(t), (TILES * h + t) % 3, :]
                    nc.scalar.activation(a, a, ACT.Exp).then_inc(exped, 1)

                def take_context(b, h):
                    act.wait_ge(pv_done, b * STEPS + TILES * (h + 1))
                    act.wait_ge(ctx_stored[h % 2], (b * PAIRS + h // 2) * 32)
                    nc.scalar.activation(halves(ctx_sb[:, h % 2, S - 1::-1]), ct[:, :, 0:HALF],
                                         ACT.Copy).then_inc(ctx_copied, 1)

                def store_context(b, h):
                    r = DK * (h % 2)
                    act.wait_ge(ctx_copied, b * NH + (h + 1))
                    act.dma_start(dram["ctx"][h * DK:(h + 1) * DK, bass.ds(b * S, S)], ctx_sb[r:r + DK, h % 2, :])\
                       .then_inc(ctx_stored[h % 2], 16)
                    act.dma_start(dram["sums"][h:h + 1, bass.ds(b * S, S)], ctx_sb[DK - r:DK - r + 1, h % 2, :])\
                       .then_inc(ctx_stored[h % 2], 16)

                act.wait_ge(constants_set, 1)
                act.wait_ge(small_landed, 48)
                nc.scalar.mul(b_qk[:, 0], b_qk[:, 0], SCALE).then_inc(small_landed, 1)
                act.wait_ge(small_landed, 49)
                with act.Fori(0, images) as b:
                    stage(b, 0, 0)
                    stage(b, 1, 0)
                    upper(b, 0, 0)
                    upper(b, 0, 1)
                    for h in range(NH):
                        c = stages_pair(h)
                        if h + 1 < NH:
                            upper(b, h + 1, 0)
                        for t in range(TILES):
                            exponentials(b, h, t)
                            if t == 0 and h:
                                take_context(b, h - 1)
                            if t == 0 and c is not None:
                                stage(b, 0, c)
                            if t == 1 and c is not None:
                                stage(b, 1, c)
                            if t == 1 and h:
                                store_context(b, h - 1)
                            if t == 2 and h + 1 < NH:
                                upper(b, h + 1, 1)
                    take_context(b, NH - 1)
                    store_context(b, NH - 1)
                for stored in ctx_stored:
                    act.wait_ge(stored, images * PAIRS * 32)

            @block.vector
            def _(dve):
                def take_v(b, t):
                    dve.wait_ge(v_ready, b * TILES + (t + 1))
                    m = tile_rows(t)
                    src = st[t // 2 % 2][0:m, t % 2, :].rearrange("p (c e n) -> p c e n", e=2, n=DK)
                    nc.vector.tensor_tensor(v[0:m, t, :, 0:3:2, :], src,
                                            bv[0:m, :].rearrange("p (c e n) -> p c e n", e=2, n=DK),
                                            ALU.add).then_inc(v_staged, 1)

                def first_max(b, h, t):
                    dve.wait_ge(first_ready, b * STEPS + (TILES * h + t + 1))
                    dve.sem_inc(first_seen, 1)
                    top = (SHIFTS - ROWS + 1 - ROWS * t) * GRID + GRID - 1
                    nc.vector.tensor_tensor_reduce(s1[0:TILE, :, 0:HALF], s1[0:TILE, :, 0:HALF], window(h, TILE, top),
                                                   1.0, -3e38, ALU.add, ALU.max, maxima[:, t:t + 1]).then_inc(maxed, 1)

                def spread_max(b, h):
                    dve.wait_ge(turned, b * NH + (h + 1))
                    a = s1[0:TILES, 0:1, 0:TILE].to_broadcast([TILES, TILES, TILE])
                    nc.vector.tensor_tensor(q_lom[DK:DK + TILES, h % 2, :].rearrange("p (a n) -> p a n", a=TILES),
                                            a, spread[:, :, :], ALU.mult).then_inc(max_spread, 1)

                def add_bias(b, h, t):
                    s = TILES * h + t
                    dve.wait_ge(scores_ready, b * STEPS + (s + 1))
                    dve.wait_ge(pv_done, b * STEPS + (s - 2 if s >= 3 else 0))
                    m = tile_rows(t)
                    top = ROWS * (TILES - 1 - t) * GRID + S - 1
                    nc.vector.tensor_tensor(halves(probs[0:m, s % 3, :]), st[s % 2][0:m, :, 0:HALF], window(h, m, top),
                                            ALU.add).then_inc(biased, 1)

                dve.wait_ge(constants_set, 1)
                dve.wait_ge(small_landed, 48)
                with dve.Fori(0, images) as b:
                    dve.wait_ge(pv_done, b * STEPS)
                    for t in range(TILES):
                        take_v(b, t)
                        if t >= 4:
                            first_max(b, 0, 2 * t - 8)
                            first_max(b, 0, 2 * t - 7)
                    spread_max(b, 0)
                    for h in range(NH):
                        for t in range(TILES):
                            add_bias(b, h, t)
                            if h + 1 < NH:
                                for i in FIRST[t]:
                                    first_max(b, h + 1, i)
                        if h + 1 < NH:
                            spread_max(b, h + 1)

            @block.tensor
            def _(pe):
                def project(b, i, c):
                    if i == 0:
                        pe.wait_ge(wqk_landed, (b * PAIRS + (c + 1)) * 16)
                        pe.wait_ge(max_spread, b * NH + (2 * c - 1 if c else 0))
                    else:
                        pe.wait_ge(qk_staged, b * (2 * PAIRS) + (2 * c + 1))
                    for k in range(KC):
                        for w, xs in ((0, x_hi), (0, x_lo), (1, x_hi)):
                            for n in range(2):
                                mm = nc.tensor.matmul(s1[:, n, 0:HALF], w_qk[:, i, w, k, :],
                                                      xs[:, k, n * HALF:(n + 1) * HALF],
                                                      start=(k == 0 and w == 0 and xs is x_hi),
                                                      stop=(k == KC - 1 and w == 1))
                    mm.then_inc(qk_ready, 1)

                def project_v(b, t):
                    m = tile_rows(t)
                    if t < 4:
                        pe.wait_ge(biased, b * STEPS)
                    else:
                        pe.wait_ge(v_staged, b * TILES + (t - 3))
                    for k in range(KC):
                        for xs, w in ((x_hi, wv_hi), (x_hi, wv_lo), (x_lo, wv_hi)):
                            mm = nc.tensor.matmul(st[t // 2 % 2][0:m, t % 2, :], xs[:, k, t * TILE:t * TILE + m], w[:, k, :],
                                                  start=(k == 0 and xs is x_hi and w is wv_hi),
                                                  stop=(k == KC - 1 and xs is x_lo))
                    mm.then_inc(v_ready, 1)

                def first_scores(b, h, t):
                    s = h % 2
                    if t == 0:
                        pe.wait_ge(head_hi, b * NH + (h + 1))
                        pe.wait_ge(qk_staged, b * (2 * PAIRS) + 2 * min(PAIRS, (h + 1) // 2 + 1 if h else 1))
                        if h:
                            pe.wait_ge(max_spread, b * NH + h)
                    else:
                        pe.wait_ge(maxed, b * STEPS + (TILES * h + t))
                    for n in range(2):
                        mm = nc.tensor.matmul(s1[0:TILE, n, 0:HALF], q_hi2[0:DK, s, t * TILE:(t + 1) * TILE],
                                              k_hilo[0:DK, s, n * HALF:(n + 1) * HALF], start=True, stop=True)
                    mm.then_inc(first_ready, 1)

                def turn_max(b, h):
                    pe.wait_ge(maxed, b * STEPS + TILES * (h + 1))
                    nc.tensor.matmul(s1[0:TILES, 0, 0:TILE], maxima[:, :], ident[:, :], start=True, stop=True)\
                      .then_inc(turned, 1)

                def scores(b, h, t):
                    s, m, i = h % 2, tile_rows(t), TILES * h + t
                    if t == 0:
                        pe.wait_ge(lo_split, b * NH + (h + 1))
                        pe.wait_ge(max_spread, b * NH + (h + 1))
                    if i < 2:
                        pe.wait_ge(v_staged, b * TILES + TILES)
                    else:
                        pe.wait_ge(biased, b * STEPS + (i - 1))
                    for n in range(2):
                        q = slice(n * HALF, (n + 1) * HALF)
                        nc.tensor.matmul(st[i % 2][0:m, n, 0:HALF], k_hilo[:, s, t * TILE:t * TILE + m], q_hi2[:, s, q],
                                         start=True, stop=False)
                    for n in range(2):
                        q = slice(n * HALF, (n + 1) * HALF)
                        mm = nc.tensor.matmul(st[i % 2][0:m, n, 0:HALF], k_hi1[:, s, t * TILE:t * TILE + m], q_lom[:, s, q],
                                              start=False, stop=True)
                    mm.then_inc(scores_ready, 1)

                def weigh_values(b, h, t):
                    m, i = tile_rows(t), TILES * h + t
                    pe.wait_ge(exped, b * STEPS + (i + 1))
                    if t == 0:
                        pe.wait_ge(ctx_copied, b * NH + h)
                    e = h % 2
                    vs = v[0:m, t, h // 2, e:e + 2, :].rearrange("p a n -> p (a n)")
                    for n in range(2):
                        mm = nc.tensor.matmul(ct[:, n, 0:HALF], vs, probs[0:m, i % 3, n * HALF:(n + 1) * HALF],
                                              start=(t == 0), stop=(t == TILES - 1))
                    mm.then_inc(pv_done, 1)

                pe.wait_ge(constants_set, 1)
                with pe.Fori(0, images) as b:
                    pe.wait_ge(x_split, b * KC + KC)
                    project(b, 0, 0)
                    project(b, 1, 0)
                    for t in range(TILES):
                        project_v(b, t)
                        if t >= 4:
                            first_scores(b, 0, 2 * t - 8)
                            first_scores(b, 0, 2 * t - 7)
                    turn_max(b, 0)
                    for h in range(NH):
                        c = stages_pair(h)
                        for t in range(TILES):
                            scores(b, h, t)
                            if t < 2 and c is not None:
                                project(b, t, c)
                            for i in FIRST[t][:1] if h + 1 < NH else ():
                                first_scores(b, h + 1, i)
                            if t:
                                weigh_values(b, h, t - 1)
                            for i in FIRST[t][1:] if h + 1 < NH else ():
                                first_scores(b, h + 1, i)
                        if h + 1 < NH:
                            turn_max(b, h + 1)
                        weigh_values(b, h, TILES - 1)


TOKENS = IMAGES * S
SUB = 120
SUBS = 3
TT = SUB * SUBS
NT = TOKENS // TT
NEWTON = 3
RSQRT_MAGIC = 0x5F3759DF


def feed_forward(nc, dram):
    with ExitStack() as ctx:
        def sb(name, shape, dt=F32):
            return ctx.enter_context(nc.sbuf_tensor(name, shape, dt))

        def ps(name, shape):
            return ctx.enter_context(nc.psum_tensor(name, shape, F32))

        def sem(name):
            return ctx.enter_context(nc.semaphore(name))

        wo = [sb(f"wo_{p}", [P, KC, D], F32R) for p in ("hi", "lo")]
        w1 = [sb(f"w1_{p}", [P, KC, FF], F32R) for p in ("hi", "lo")]
        w2 = [sb(f"w2_{p}", [P, FC, D], F32R) for p in ("hi", "lo")]
        bo_row, g1_row, be1_row, g2_row, be2_row = (sb(n, [SUB, D]) for n in ("bo_row", "g1_row", "be1_row", "g2_row", "be2_row"))
        b1_col = sb("b1_col", [P, FC])
        g1_col = sb("g1_col", [P, KC])
        be1_col = sb("be1_col", [P, KC])
        ident = sb("ident2", [SUB, SUB])
        y_ps = ps("y_ps", [P, SUBS, 512])
        h_ps = ps("h_ps", [P, 2, 512])
        z_ps = ps("z_ps", [P, SUBS, 512])

        weights_landed = [sem("weights_landed0"), sem("weights_landed1")]
        weights_hi = sem("weights_hi")
        weights_lo = sem("weights_lo")
        rows_landed = sem("rows_landed")
        b2_landed = sem("b2_landed")
        rows_added = sem("rows_added")
        sums_landed = sem("sums_landed")
        inverted = sem("inverted")
        inverse_stored = sem("inverse_stored")
        ident_set = sem("ident_set")

        with ExitStack() as early:
            raw = early.enter_context(nc.sbuf_tensor("raw2", [P, 2, FF], F32))
            sums = early.enter_context(nc.sbuf_tensor("sums_sb", [P, NH * TOKENS // P], F32))
            b2_row = early.enter_context(nc.sbuf_tensor("b2_row", [SUB, D], F32))
            parts = [(dram["w_o"].rearrange("(k p) n -> p k n", p=P), wo, slice(0, KC))]
            parts += [(dram["w1"][k * P:(k + 1) * P, :], w1, k) for k in range(KC)]
            w2_view = dram["w2"].rearrange("(f p) n -> p f n", p=P)
            parts += [(w2_view[:, 4 * j:4 * j + 4, :], w2, slice(4 * j, 4 * j + 4)) for j in range(4)]

            def raw_view(n, at):
                a = raw[:, n % 2, :]
                return a if isinstance(at, int) else a.rearrange("p (k n) -> p k n", n=D)

            with nc.Block() as block:
                @block.sync
                def _(sp):
                    sp.dma_start(sums[:, :], dram["sums"].rearrange("h (a n) -> (h a) n", a=P // NH)).then_inc(sums_landed, 16)
                    for row, name in ((bo_row, "b_o"), (g1_row, "ln1_g"), (be1_row, "ln1_b"), (g2_row, "ln2_g"),
                                      (be2_row, "ln2_b"), (b2_row, "b2")):
                        sp.dma_start(row[:, :], dram[name].to_broadcast([SUB, D])).then_inc(rows_landed, 16)
                    for col, name in ((b1_col, "b1"), (g1_col, "ln1_g_col"), (be1_col, "ln1_b_col")):
                        sp.dma_start(col[:, :], dram[name]).then_inc(rows_landed, 16)
                    for n, (src, _, at) in enumerate(parts):
                        if n >= 2:
                            sp.wait_ge(weights_lo, n - 1)
                        sp.dma_start(raw_view(n, at), src).then_inc(weights_landed[n % 2], 16)
                    sp.wait_ge(inverted, 1)
                    sp.dma_start(dram["inverse"].rearrange("h (a n) -> (h a) n", a=P // NH), sums[:, :])\
                      .then_inc(inverse_stored, 16)
                    sp.wait_ge(inverse_stored, 16)
                    sp.wait_ge(rows_landed, 16 * 9)

                @block.scalar
                def _(act):
                    for n, (_, to, at) in enumerate(parts):
                        act.wait_ge(weights_landed[n % 2], 16 * (n // 2 + 1))
                        nc.scalar.activation(to[0][:, at], raw_view(n, at), ACT.Copy).then_inc(weights_hi, 1)

                @block.vector
                def _(dve):
                    dve.wait_ge(sums_landed, 16)
                    nc.vector.reciprocal(sums[:, :], sums[:, :]).then_inc(inverted, 1)
                    for n, (_, to, at) in enumerate(parts):
                        dve.wait_ge(weights_hi, n + 1)
                        nc.vector.tensor_tensor(to[1][:, at], raw_view(n, at), to[0][:, at].bitcast(F32),
                                                ALU.subtract).then_inc(weights_lo, 1)

                @block.gpsimd
                def _(pool):
                    nc.gpsimd.memset(ident[:, :], 0.0).then_inc(ident_set, 1)
                    pool.wait_ge(ident_set, 1)
                    nc.gpsimd.affine_select(out=ident[:, :], in_=ident[:, :], compare_op=ALU.not_equal, fill=1.0,
                                            base=0, pattern=[[-1, SUB]], channel_multiplier=1).then_inc(ident_set, 1)
                    pool.wait_ge(rows_landed, 16 * 9)
                    nc.gpsimd.tensor_tensor(be1_row[:, :], be1_row[:, :], b2_row[:, :], ALU.add).then_inc(rows_added, 1)

        c_raw = sb("c_raw", [P, 2, TT])
        c_inv = sb("c_inv", [P, 2, TT])
        c_t = [sb(f"c_{p}", [P, KC, TT], F32R) for p in ("hi", "lo")]
        res = sb("res", [SUB, 2, SUBS, D])
        a_t = [sb(f"a_{p}", [P, KC, TT], F32R) for p in ("hi", "lo")]
        g = sb("g", [P, 2, TT])
        h_t = [sb(f"h_{p}", [P, 2, TT], F32R) for p in ("hi", "lo")]
        stats = sb("stats", [SUB, 6])
        mean_var = sb("mean_var", [SUB, 2])
        var = sb("var", [SUB, 1])
        root = sb("root", [SUB, 1])
        step = sb("step", [SUB, 1])

        ctx_landed = [sem("ctx_landed0"), sem("ctx_landed1")]
        sp_passed = sem("sp_passed")
        divided = sem("divided")
        ctx_hi = sem("ctx_hi")
        ctx_split = sem("ctx_split")
        x_landed = [sem("x_landed_even"), sem("x_landed_odd")]
        x_biased = sem("x_biased")
        z_ready = sem("z_ready")
        z_taken = sem("z_taken")
        ln_step = sem("ln_step")
        ln_passed = sem("ln_passed")
        normed1 = sem("normed1")
        normed2 = sem("normed2")
        turned = sem("turned2")
        turn_staged = sem("turn_staged")
        a_hi = sem("a_hi")
        a_split = sem("a_split")
        h_ready = sem("h_ready")
        g_done = sem("g_done")
        h_hi = sem("h_hi")
        h_split = sem("h_split")
        y_step = sem("y_step")
        y_taken = sem("y_taken")
        scaled = sem("scaled")
        residual_ready = sem("residual_ready")
        out_ready = sem("out_ready")
        out_stored = [sem("out_stored_even"), sem("out_stored_odd")]
        LN_OPS = 5 + 3 * NEWTON

        def tiles(eng, front, body, tail):
            front(0, 0, 0)
            body(0, 0, 0, False, True)
            with eng.Fori(0, (NT - 2) // 2) as u:
                body(u * 2 + 1, u, 1, True, True)
                body(u * 2 + 2, u + 1, 0, True, True)
            body(NT - 1, (NT - 1) // 2, 1, True, False)
            tail(NT - 1, 1)

        def nothing(*_):
            return None

        with nc.Block() as block:
            @block.sync
            def _(sp):
                def load_context(t):
                    for c in range(KC):
                        sp.wait_ge(ctx_split, t * KC + (c - 1 if c >= 2 else 0))
                        sp.sem_inc(sp_passed, 1)
                        sp.dma_start(c_raw[:, c % 2], dram["ctx"][c * P:(c + 1) * P, bass.ds(t * TT, TT)])\
                          .then_inc(ctx_landed[c % 2], 16)
                        for i in range(2):
                            sp.dma_start(c_inv[i * DK:(i + 1) * DK, c % 2],
                                         dram["inverse"][2 * c + i:2 * c + i + 1, bass.ds(t * TT, TT)].to_broadcast([DK, TT]))\
                              .then_inc(ctx_landed[c % 2], 16)

                def load_x(t, u, e):
                    sp.wait_ge(out_stored[e], u * 16)
                    sp.dma_start(res[:, e], dram["x"][bass.ds(t * TT, TT), :].rearrange("(s p) n -> p s n", p=SUB))\
                      .then_inc(x_landed[e], 16)

                def front(t, u, e):
                    load_context(t)
                    load_x(t, u, e)

                def store(t, e):
                    sp.wait_ge(out_ready, t + 1)
                    sp.dma_start(dram["out"][bass.ds(t * TT, TT), :].rearrange("(s p) n -> p s n", p=SUB), res[:, e])\
                      .then_inc(out_stored[e], 16)

                def body(t, u, e, has_prev, has_next):
                    if has_next:
                        load_context(t + 1)
                    if has_prev:
                        store(t - 1, 1 - e)
                    if has_next:
                        load_x(t + 1, u + e, 1 - e)

                tiles(sp, front, body, store)
                sp.wait_ge(out_stored[0], NT // 2 * 16)
                sp.wait_ge(out_stored[1], NT // 2 * 16)

            @block.gpsimd
            def _(pool):
                def divide_context(t):
                    for c in range(KC):
                        pool.wait_ge(ctx_landed[c % 2], (t * 2 + (c // 2 + 1)) * 48)
                        nc.gpsimd.tensor_tensor(c_raw[:, c % 2], c_raw[:, c % 2], c_inv[:, c % 2], ALU.mult).then_inc(divided, 1)
                        pool.wait_ge(z_ready, t * SUBS)
                        pool.wait_ge(ctx_hi, t * KC + (c + 1))
                        nc.gpsimd.tensor_tensor(c_t[1][:, c], c_raw[:, c % 2], c_t[0][:, c].bitcast(F32),
                                                ALU.subtract).then_inc(ctx_split, 1)

                def bias_x(u, e):
                    pool.wait_ge(x_landed[e], (u + 1) * 16)
                    for s in range(SUBS):
                        nc.gpsimd.tensor_tensor(res[:, e, s], res[:, e, s], bo_row[:, :], ALU.add).then_inc(x_biased, 1)

                def scale_and_shift(n, e, g_row, b_row, done):
                    for s in range(SUBS):
                        nc.gpsimd.tensor_tensor(res[:, e, s], res[:, e, s], g_row[:, :], ALU.mult).then_inc(scaled, 1)
                    pool.wait_ge(scaled, n * SUBS + SUBS)
                    for s in range(SUBS):
                        i = nc.gpsimd.tensor_tensor(res[:, e, s], res[:, e, s], b_row[:, :], ALU.add)
                    i.then_inc(done, 1)

                def body(t, u, e, has_prev, has_next):
                    if has_next:
                        divide_context(t + 1)
                    if has_prev:
                        pool.wait_ge(normed2, t * SUBS)
                        scale_and_shift(t * 2, 1 - e, g2_row, be2_row, out_ready)
                    if has_next:
                        bias_x(u + e, 1 - e)
                        pool.wait_ge(turned, t * KC + 2 * KC)
                        scale_and_shift(t * 2 + 1, 1 - e, g1_row, be1_row, residual_ready)

                def first(t, u, e):
                    divide_context(t)
                    bias_x(u, e)
                    pool.wait_ge(turned, KC)
                    scale_and_shift(0, e, g1_row, be1_row, residual_ready)

                def tail(t, e):
                    pool.wait_ge(normed2, NT * SUBS)
                    scale_and_shift(2 * NT - 1, e, g2_row, be2_row, out_ready)

                tiles(pool, first, body, tail)

            @block.scalar
            def _(act):
                def context_upper(t):
                    for c in range(KC):
                        act.wait_ge(z_ready, t * SUBS)
                        act.wait_ge(divided, t * KC + (c + 1))
                        nc.scalar.activation(c_t[0][:, c], c_raw[:, c % 2], ACT.Copy).then_inc(ctx_hi, 1)

                def take_turned(t):
                    for c in range(KC):
                        act.wait_ge(turned, t * KC + (c + 1))
                        if c < 2:
                            act.wait_ge(h_split, t * FC)
                        else:
                            act.wait_ge(a_split, t * KC + (c - 1))
                        nc.scalar.activation(g[:, c % 2], z_ps[:, c % SUBS, 0:TT], ACT.Identity, bias=be1_col[:, c:c + 1],
                                             scale=g1_col[:, c:c + 1]).then_inc(turn_staged, 1)
                        act.wait_ge(h_ready, t * FC)
                        act.wait_ge(turn_staged, t * KC + (c + 1))
                        nc.scalar.activation(a_t[0][:, c], g[:, c % 2], ACT.Copy).then_inc(a_hi, 1)

                def gelu(t, f):
                    act.wait_ge(h_ready, t * FC + (f + 1))
                    if f < 2:
                        act.wait_ge(a_split, t * KC + KC)
                    else:
                        act.wait_ge(h_split, t * FC + (f - 1))
                    nc.scalar.activation(g[:, f % 2], h_ps[:, f % 2, 0:TT], ACT.Gelu, bias=b1_col[:, f:f + 1])\
                      .then_inc(g_done, 1)
                    act.wait_ge(y_step, t * FC + (f - 1 if f >= 2 else 0))
                    act.wait_ge(g_done, t * FC + (f + 1))
                    nc.scalar.activation(h_t[0][:, f % 2], g[:, f % 2], ACT.Copy).then_inc(h_hi, 1)

                def front(t, u, e):
                    context_upper(t)
                    take_turned(t)

                def body(t, u, e, has_prev, has_next):
                    for f in range(FC):
                        gelu(t, f)
                        if f == 2 and has_next:
                            context_upper(t + 1)
                    if has_next:
                        take_turned(t + 1)

                tiles(act, front, body, nothing)

            @block.vector
            def _(dve):
                def layer_norm(q, a, done):
                    n = [0]

                    def then(i):
                        i.then_inc(ln_step, 1)
                        n[0] += 1
                        dve.wait_ge(ln_step, q * LN_OPS + n[0])

                    then(nc.vector.bn_stats(stats[:, :], a))
                    dve.sem_inc(ln_passed, 1)
                    then(nc.vector.bn_aggr(mean_var[:, :], stats[:, :]))
                    then(nc.vector.tensor_scalar(var[:, :], mean_var[:, 1:2], LN_EPS, None, ALU.add))
                    then(nc.vector.tensor_scalar(root[:, :].bitcast(I32), var[:, :].bitcast(I32), 1, None,
                                                 ALU.logical_shift_right))
                    then(nc.vector.tensor_scalar(root[:, :].bitcast(I32), root[:, :].bitcast(I32), -1.0, float(RSQRT_MAGIC),
                                                 ALU.mult, ALU.add))
                    for _ in range(NEWTON):
                        then(nc.vector.tensor_scalar(step[:, :], root[:, :], root[:, :], var[:, :], ALU.mult, ALU.mult))
                        then(nc.vector.tensor_scalar(step[:, :], step[:, :], -0.5, 1.5, ALU.mult, ALU.add))
                        then(nc.vector.tensor_scalar(root[:, :], root[:, :], step[:, :], None, ALU.mult))
                    nc.vector.tensor_scalar(a, a, mean_var[:, 0:1], root[:, :], ALU.subtract, ALU.mult).then_inc(done, 1)

                def first_norm(q, t, e, s):
                    dve.wait_ge(x_biased, t * SUBS + (s + 1))
                    dve.wait_ge(z_ready, t * SUBS + (s + 1))
                    nc.vector.tensor_tensor(res[:, e, s], z_ps[0:SUB, s, :], res[:, e, s], ALU.add).then_inc(z_taken, 1)
                    dve.wait_ge(z_taken, t * SUBS + (s + 1))
                    layer_norm(q, res[:, e, s], normed1)

                def a_lower(t):
                    for c in range(KC):
                        dve.wait_ge(a_hi, t * KC + (c + 1))
                        nc.vector.tensor_tensor(a_t[1][:, c], g[:, c % 2], a_t[0][:, c].bitcast(F32),
                                                ALU.subtract).then_inc(a_split, 1)

                def h_lower(t, f):
                    dve.wait_ge(h_hi, t * FC + (f + 1))
                    nc.vector.tensor_tensor(h_t[1][:, f % 2], g[:, f % 2], h_t[0][:, f % 2].bitcast(F32),
                                            ALU.subtract).then_inc(h_split, 1)

                def take_y(t, e):
                    dve.wait_ge(residual_ready, t + 1)
                    dve.wait_ge(y_step, t * FC + FC)
                    for s in range(SUBS):
                        nc.vector.tensor_tensor(res[:, e, s], y_ps[0:SUB, s, :], res[:, e, s], ALU.add).then_inc(y_taken, 1)

                def front(t, u, e):
                    for s in range(SUBS):
                        first_norm(s, 0, 0, s)
                    a_lower(0)

                def body(t, u, e, has_prev, has_next):
                    for f in range(FC):
                        h_lower(t, f)
                        if has_prev and 1 <= f < 1 + SUBS:
                            dve.wait_ge(y_taken, t * SUBS)
                            layer_norm(t * 6 + (f - 1), res[:, 1 - e, f - 1], normed2)
                        if has_next and 10 <= f < 10 + SUBS:
                            first_norm(t * 6 + (f - 10 + 3), t + 1, 1 - e, f - 10)
                    if has_next:
                        a_lower(t + 1)
                    take_y(t, e)

                def tail(t, e):
                    dve.wait_ge(y_taken, NT * SUBS)
                    for s in range(SUBS):
                        layer_norm((NT - 1) * 6 + 3 + s, res[:, e, s], normed2)

                tiles(dve, front, body, tail)

            @block.tensor
            def _(pe):
                PASSES = ((0, 0), (0, 1), (1, 0))

                def project_out(t, s):
                    if s == 0:
                        pe.wait_ge(ctx_split, t * KC + KC)
                        pe.wait_ge(turn_staged, t * KC)
                    for k in range(KC):
                        for x, w in PASSES:
                            mm = nc.tensor.matmul(z_ps[0:SUB, s, :], c_t[x][:, k, s * SUB:(s + 1) * SUB], wo[w][:, k, :],
                                                  start=(k + x + w == 0), stop=(k == KC - 1 and x == 1))
                    mm.then_inc(z_ready, 1)

                def turn(t, e, c):
                    if c == 0:
                        pe.wait_ge(normed1, t * SUBS + SUBS)
                    if c >= SUBS:
                        pe.wait_ge(turn_staged, t * KC + (c - SUBS + 1))
                    for s in range(SUBS):
                        mm = nc.tensor.transpose(z_ps[:, c % SUBS, s * SUB:(s + 1) * SUB], res[:, e, s, c * P:(c + 1) * P],
                                                 ident[:, :])
                    mm.then_inc(turned, 1)

                def widen(t, f):
                    if f == 0:
                        pe.wait_ge(a_split, t * KC + KC)
                    pe.wait_ge(g_done, t * FC + (f - 1 if f >= 2 else 0))
                    for k in range(KC):
                        for x, w in ((0, 0), (1, 0), (0, 1)):
                            mm = nc.tensor.matmul(h_ps[:, f % 2, 0:TT], w1[w][:, k, f * P:(f + 1) * P], a_t[x][:, k, :],
                                                  start=(k + x + w == 0), stop=(k == KC - 1 and w == 1))
                    mm.then_inc(h_ready, 1)

                def narrow(t, f):
                    pe.wait_ge(h_split, t * FC + (f + 1))
                    if f == 0:
                        pe.wait_ge(y_taken, t * SUBS)
                    for s in range(SUBS):
                        for x, w in PASSES:
                            mm = nc.tensor.matmul(y_ps[0:SUB, s, :], h_t[x][:, f % 2, s * SUB:(s + 1) * SUB], w2[w][:, f, :],
                                                  start=(f + x + w == 0), stop=(f == FC - 1 and x == 1))
                    mm.then_inc(y_step, 1)

                def front(t, u, e):
                    for s in range(SUBS):
                        project_out(0, s)
                    for c in range(KC):
                        turn(0, 0, c)

                def body(t, u, e, has_prev, has_next):
                    for f in range(FC):
                        widen(t, f)
                        if f == FC - 1 and has_next:
                            for c in range(SUBS):
                                turn(t + 1, 1 - e, c)
                        if f:
                            narrow(t, f - 1)
                        if 7 <= f < 7 + SUBS and has_next:
                            project_out(t + 1, f - 7)
                    if has_next:
                        turn(t + 1, 1 - e, SUBS)
                    narrow(t, FC - 1)

                tiles(pe, front, body, nothing)


def build(nc, dram, images=IMAGES):
    with ExitStack() as ctx:
        bias = ctx.enter_context(nc.sbuf_tensor("bias", [TILE, NH, WINDOW], F32))
        wv_hi = ctx.enter_context(nc.sbuf_tensor("wv_hi", [P, KC, D], F32R))
        wv_lo = ctx.enter_context(nc.sbuf_tensor("wv_lo", [P, KC, D], F32R))
        prepare_tables(nc, dram, bias, wv_hi, wv_lo)
        attention(nc, dram, bias, wv_hi, wv_lo, images)
    feed_forward(nc, dram)


def displacement_onehot():
    import numpy as np

    r, c = np.indices((UROWS, UCOLS))
    dh = (GRID + 1 - r).astype(np.float64)
    dw = (GRID - 1 - c).astype(np.float64)
    dist = np.minimum(np.sqrt(dh ** 2 + dw ** 2).astype(np.int64), DISTS - 1)
    direction = ((np.arctan2(dh, dw) + np.pi) / (2.0 * np.pi) * DIRS).astype(np.int64) % DIRS
    direction = np.where((dh == 0) & (dw == 0), 0, direction)
    out = np.zeros((DISTS + DIRS, r.size), np.float32)
    out[dist.ravel(), np.arange(r.size)] = 1.0
    out[DISTS + direction.ravel(), np.arange(r.size)] = 1.0
    return out


def kernel(**inputs):
    import numpy as np
    import concourse.bacc as bacc
    from concourse.bass_utils import run_bass_kernel_spmd

    def given(name):
        return np.ascontiguousarray(inputs[name if name == "x" else "L0_conv_" + name])

    def columns(name):
        return np.ascontiguousarray(given(name).reshape(-1, P).T)

    x = given("x").reshape(TOKENS, D)
    arrays = {"x": x, "x_t": np.ascontiguousarray(x.T), "displacement_onehot": displacement_onehot()}
    for name in ("dist_bias", "dir_bias", "w_q", "w_k", "w_v", "w_o", "w1", "w2"):
        arrays[name] = given(name)
    for name in ("b_q", "b_k", "b1"):
        arrays[name] = columns(name)
    for name in ("b_v", "b_o", "b2", "ln1_g", "ln1_b", "ln2_g", "ln2_b"):
        arrays[name] = given(name).reshape(1, D)
    for name in ("ln1_g", "ln1_b"):
        arrays[name + "_col"] = columns(name)

    nc = bacc.Bacc("TRN2", target_bir_lowering=False, num_devices=1)
    dram = {name: nc.dram_tensor(name, a.shape, mybir.dt.from_np(a.dtype), kind="ExternalInput").ap()
            for name, a in arrays.items()}
    for name, shape in (("skew", (NH, GRID, UROWS * GRID)), ("qk_weights", (PAIRS, P, 4 * KC * P)),
                        ("ctx", (D, TOKENS)), ("sums", (NH, TOKENS)), ("inverse", (NH, TOKENS))):
        dram[name] = nc.dram_tensor(name, shape, F32, kind="Internal").ap()
    dram["out"] = nc.dram_tensor("out", (TOKENS, D), F32, kind="ExternalOutput").ap()
    build(nc, dram)
    got = run_bass_kernel_spmd(nc, [arrays], core_ids=[0])
    return got.results[0]["out"].reshape(IMAGES, GRID, GRID, D)
```

```python
from contextlib import ExitStack

import concourse.bass as bass
from concourse import mybir

F32 = mybir.dt.float32
F32R = mybir.dt.float32r
I32 = mybir.dt.int32
ALU = mybir.AluOpType
ACT = mybir.ActivationFunctionType

P = 128
IMAGES, GRID, D = 8, 30, 512
S = GRID * GRID
NH = 8
DK = D // NH
FF = 2048
KC = D // P
PAIRS = NH // 2
FC = FF // P
LN_EPS = 1e-5
DISTS, DIRS = 60, 16

ROWS = 4
TILE = ROWS * GRID
TILES = -(-GRID // ROWS)
LAST = S - (TILES - 1) * TILE
SPAD = TILES * TILE
HALF = S // 2
SHIFTS = GRID + ROWS * (TILES - 1) + 2
UROWS, UCOLS = SHIFTS + ROWS - 1, 2 * GRID - 1
WINDOW = SHIFTS * GRID
SCALE = DK ** -0.5


def tile_rows(t):
    return TILE if t < TILES - 1 else LAST


def prepare_tables(nc, dram, bias, wv_hi, wv_lo):
    with ExitStack() as ctx:
        def sb(name, shape, dt=F32):
            return ctx.enter_context(nc.sbuf_tensor(name, shape, dt))

        def sem(name):
            return ctx.enter_context(nc.semaphore(name))

        CH = 413
        NCH = UROWS * UCOLS // CH
        assert NCH * CH == UROWS * UCOLS
        table = sb("table", [DISTS + DIRS, NH])
        onehot = sb("onehot", [DISTS + DIRS, UROWS * UCOLS])
        u_sb = sb("u_sb", [NH, UROWS * UCOLS])
        raw = sb("raw", [P, 3, KC, D])
        qk_split = sb("qk_split", [P, PAIRS, 2, 2, KC, P], F32R)
        u_ps = ctx.enter_context(nc.psum_tensor("u_ps", [P, 4, 512], F32))

        table_landed = sem("table_landed")
        raw_landed = sem("raw_landed")
        u_ready = sem("u_ready")
        u_copied = sem("u_copied")
        skew_stored = sem("skew_stored")
        bias_landed = sem("bias_landed")
        w_hi_done = sem("w_hi_done")
        w_lo_done = sem("w_lo_done")
        qk_stored = sem("qk_stored")
        u_view = u_sb[:, :].rearrange("h (r c) -> h r c", c=UCOLS)

        with nc.Block() as block:
            @block.sync
            def _(sp):
                sp.dma_start(table[0:DISTS, :], dram["dist_bias"]).then_inc(table_landed, 16)
                sp.dma_start(table[DISTS:DISTS + DIRS, :], dram["dir_bias"]).then_inc(table_landed, 16)
                sp.dma_start(onehot[:, :], dram["displacement_onehot"]).then_inc(table_landed, 16)
                for i, name in enumerate(("w_q", "w_k", "w_v")):
                    sp.dma_start(raw[:, i], dram[name].rearrange("(k p) n -> p k n", p=P)).then_inc(raw_landed, 16)
                sp.wait_ge(u_copied, NCH)
                for w in range(GRID):
                    sp.dma_start(dram["skew"][:, w].rearrange("h (r c) -> h r c", c=GRID),
                                 u_view[:, :, GRID - 1 - w:2 * GRID - 1 - w]).then_inc(skew_stored, 16)
                sp.wait_ge(skew_stored, 16 * GRID)
                for a in range(ROWS):
                    o = (ROWS - 1 - a) * GRID
                    sp.dma_start(bias[a * GRID:(a + 1) * GRID, :, :],
                                 dram["skew"][:, :, o:o + WINDOW].rearrange("h w n -> w h n")).then_inc(bias_landed, 16)
                sp.wait_ge(bias_landed, 16 * ROWS)

            @block.scalar
            def _(act):
                act.wait_ge(raw_landed, 48)
                for i in range(2):
                    for c in range(PAIRS):
                        nc.scalar.activation(qk_split[:, c, i, 0], raw[:, i, :, c * P:(c + 1) * P],
                                             ACT.Copy).then_inc(w_hi_done, 1)
                nc.scalar.activation(wv_hi[:, :, :], raw[:, 2], ACT.Copy).then_inc(w_hi_done, 1)
                act.wait_ge(w_lo_done, 2 * PAIRS)
                act.dma_start(dram["qk_weights"].rearrange("c p n -> p c n"),
                              qk_split[:, :, :, :, :, :].rearrange("p c i s k n -> p c (i s k n)").bitcast(F32)).then_inc(qk_stored, 16)
                act.wait_ge(qk_stored, 16)

            @block.vector
            def _(dve):
                for j in range(NCH):
                    dve.wait_ge(u_ready, j + 1)
                    nc.vector.tensor_copy(u_sb[:, j * CH:(j + 1) * CH], u_ps[0:NH, j % 4, 0:CH]).then_inc(u_copied, 1)
                n = 0
                for i in range(2):
                    for c in range(PAIRS):
                        n += 1
                        dve.wait_ge(w_hi_done, n)
                        nc.vector.tensor_tensor(qk_split[:, c, i, 1], raw[:, i, :, c * P:(c + 1) * P],
                                                qk_split[:, c, i, 0].bitcast(F32), ALU.subtract).then_inc(w_lo_done, 1)
                dve.wait_ge(w_hi_done, n + 1)
                nc.vector.tensor_tensor(wv_lo[:, :, :], raw[:, 2], wv_hi[:, :, :].bitcast(F32),
                                        ALU.subtract).then_inc(w_lo_done, 1)

            @block.tensor
            def _(pe):
                pe.wait_ge(table_landed, 48)
                for j in range(NCH):
                    if j >= 4:
                        pe.wait_ge(u_copied, j - 3)
                    nc.tensor.matmul(u_ps[0:NH, j % 4, 0:CH], table[:, :], onehot[:, j * CH:(j + 1) * CH],
                                     start=True, stop=True).then_inc(u_ready, 1)


def attention(nc, dram, bias, wv_hi, wv_lo, images):
    with ExitStack() as ctx:
        def sb(name, shape, dt=F32):
            return ctx.enter_context(nc.sbuf_tensor(name, shape, dt))

        def ps(name):
            return ctx.enter_context(nc.psum_tensor(name, [P, 2, 512], F32))

        def sem(name):
            return ctx.enter_context(nc.semaphore(name))

        x_raw = sb("x_raw", [P, 2, S])
        x_hi = sb("x_hi", [P, KC, S], F32R)
        x_lo = sb("x_lo", [P, KC, S], F32R)
        w_qk = sb("w_qk", [P, 2, 2, KC, P], F32R)
        v = sb("v", [TILE, TILES, PAIRS, 3, DK])
        probs = sb("probs", [TILE, 3, S])
        q_f = sb("q_f", [P, 2, S])
        k_f = sb("k_f", [P, 2, S])
        q_hi2 = sb("q_hi2", [P, 2, SPAD], F32R)
        k_hilo = sb("k_hilo", [P, 2, S], F32R)
        k_hi1 = sb("k_hi1", [DK + TILES, 2, S], F32R)
        q_lom = sb("q_lom", [DK + TILES, 2, SPAD], F32R)
        ctx_sb = sb("ctx_sb", [P, 2, S])
        maxima = sb("maxima", [TILE, TILES])
        b_qk = sb("b_qk", [P, 2, PAIRS])
        bv = sb("bv", [TILE, D])
        ident = sb("ident", [TILE, TILE])
        spread = sb("spread", [TILES, TILES, TILE])
        st = [ps("st0"), ps("st1")]
        s1 = ps("s1")
        ct = ps("ct")

        x_landed = [sem("x_landed0"), sem("x_landed1")]
        x_split = sem("x_split")
        wqk_landed = sem("wqk_landed")
        small_landed = sem("small_landed")
        constants_set = sem("constants_set")
        qk_ready = sem("qk_ready")
        qk_staged = sem("qk_staged")
        head_hi = sem("head_hi")
        hi_copied = sem("hi_copied")
        lo_split = sem("lo_split")
        pool_step = sem("pool_step")
        pool_passed = sem("pool_passed")
        v_ready = sem("v_ready")
        v_staged = sem("v_staged")
        first_ready = sem("first_ready")
        first_seen = sem("first_seen")
        maxed = sem("maxed")
        turned = sem("turned")
        max_spread = sem("max_spread")
        scores_ready = sem("scores_ready")
        biased = sem("biased")
        exped = sem("exped")
        pv_done = sem("pv_done")
        ctx_copied = sem("ctx_copied")
        ctx_stored = [sem("ctx_stored0"), sem("ctx_stored1")]

        STEPS = NH * TILES
        N = None
        FIRST = {True: [(N, N, N), (N, N, N), (N, 0, N), (1, N, N), (2, N, 3), (4, N, 5), (6, N, 7), (N, N, N)],
                 False: [(N, N, N), (N, 0, N), (1, N, N), (2, N, 3), (4, N, N), (5, N, 6), (7, N, N), (N, N, N)]}
        FIRST_V = [[], [], [0, 1], [2, 3], [4, 5], [6, 7], [], []]
        TURN_V = 6
        PV_LAG = 2

        def halves(a):
            return a.rearrange("p (t n) -> p t n", t=2)

        def window(h, rows, top):
            stop = top - S
            return halves(bias[0:rows, h, top:(stop if stop >= 0 else None):-1])

        def stages_pair(h):
            return h // 2 + 1 if h % 2 == 0 and h // 2 + 1 < PAIRS else None

        from_one = [x_split, qk_ready, v_ready, lo_split, max_spread, scores_ready, biased, pv_done, ctx_copied, *ctx_stored]
        with nc.Block() as block:
            @block.sync
            def _(sp):
                for counted in from_one:
                    sp.sem_inc(counted, 1)

        with nc.Block() as block:
            @block.sync
            def _(sp):
                sp.dma_start(b_qk[:, 0], dram["b_q"]).then_inc(small_landed, 16)
                sp.dma_start(b_qk[:, 1], dram["b_k"]).then_inc(small_landed, 16)
                sp.dma_start(bv[:, :], dram["b_v"].to_broadcast([TILE, D])).then_inc(small_landed, 16)
                with sp.Fori(0, images) as b:
                    for k in range(KC):
                        if k >= 2:
                            sp.wait_ge(x_split, b * KC + (k - 1 + 1))
                        else:
                            sp.wait_ge(x_split, b * KC + 1)
                        sp.dma_start(x_raw[:, k % 2, :], dram["x_t"][k * P:(k + 1) * P, bass.ds(b * S, S)])\
                          .then_inc(x_landed[k % 2], 16)
                    for c in range(PAIRS):
                        sp.wait_ge(qk_ready, b * (2 * PAIRS) + (2 * c + 1))
                        sp.dma_start(w_qk[:, :, :, :, :].rearrange("p i s k n -> p (i s k n)").bitcast(F32),
                                     dram["qk_weights"][c]).then_inc(wqk_landed, 16)

            @block.gpsimd
            def _(pool):
                nc.gpsimd.memset(ident[:, :], 0.0).then_inc(pool_step, 1)
                nc.gpsimd.memset(spread[:, :, :], -1.0).then_inc(pool_step, 1)
                pool.wait_ge(pool_step, 2)
                nc.gpsimd.affine_select(out=ident[:, :], in_=ident[:, :], compare_op=ALU.not_equal, fill=1.0,
                                        base=0, pattern=[[-1, TILE]], channel_multiplier=1).then_inc(pool_step, 1)
                flat = spread[:, :, :].rearrange("p a n -> p (a n)")
                nc.gpsimd.affine_select(out=flat, in_=flat, compare_op=ALU.is_ge, fill=0.0, base=0,
                                        pattern=[[1, SPAD]], channel_multiplier=-TILE).then_inc(pool_step, 1)
                pool.wait_ge(pool_step, 4)
                nc.gpsimd.affine_select(out=flat, in_=flat, compare_op=ALU.is_ge, fill=0.0, base=TILE - 1,
                                        pattern=[[-1, SPAD]], channel_multiplier=TILE).then_inc(pool_step, 1)
                for t in range(TILES):
                    nc.gpsimd.memset(v[:, t, :, 1, :], 1.0).then_inc(pool_step, 1)
                pool.wait_ge(pool_step, 5 + TILES)
                nc.gpsimd.memset(q_hi2[:, :, S:SPAD].bitcast(F32), 0.0).then_inc(pool_step, 1)
                pool.wait_ge(pool_step, 6 + TILES)
                nc.gpsimd.memset(k_hi1[DK:DK + TILES, :, :].bitcast(F32), 1.0).then_inc(pool_step, 1)
                pool.wait_ge(pool_step, 7 + TILES)
                nc.gpsimd.engine_nop().then_inc(constants_set, 1)
                base = 7 + TILES
                per = KC + NH
                with pool.Fori(0, images) as b:
                    pool.wait_ge(qk_ready, b * (2 * PAIRS) + 1)
                    pool.wait_ge(v_ready, b * TILES + 1)
                    for k in range(KC):
                        pool.wait_ge(x_landed[k % 2], (b * (KC // 2) + (k // 2 + 1)) * 16)
                        pool.sem_inc(pool_passed, 1)
                        nc.gpsimd.tensor_copy(x_hi[:, k], x_raw[:, k % 2]).then_inc(pool_step, 1)
                        pool.wait_ge(pool_step, b * per + (base + k + 1))
                        nc.gpsimd.tensor_tensor(x_lo[:, k], x_raw[:, k % 2], x_hi[:, k].bitcast(F32),
                                                ALU.subtract).then_inc(x_split, 1)
                        pool.wait_ge(x_split, b * KC + (k + 2))
                    for h in range(NH):
                        s, j, r = h % 2, (h // 2) % 2, DK * (h % 2)
                        pool.wait_ge(hi_copied, b * NH + (h + 1))
                        nc.gpsimd.tensor_tensor(q_lom[0:DK, s, 0:S], q_f[r:r + DK, j], q_hi2[r:r + DK, s, 0:S].bitcast(F32),
                                                ALU.subtract).then_inc(pool_step, 1)
                        pool.wait_ge(pool_step, b * per + (base + KC + h + 1))
                        nc.gpsimd.tensor_tensor(k_hilo[DK:P, s], k_f[r:r + DK, j], k_hilo[r:r + DK, s].bitcast(F32),
                                                ALU.subtract).then_inc(lo_split, 1)
                        pool.wait_ge(lo_split, b * NH + (h + 2))

            @block.scalar
            def _(act):
                def stage(b, i, c):
                    act.wait_ge(qk_ready, b * (2 * PAIRS) + (2 * c + i + 2))
                    act.wait_ge(lo_split, b * NH + (1 + (2 * (c - 1) if c >= 2 else 0)))
                    out = halves(q_f[:, c % 2, S - 1::-1]) if i == 0 else halves(k_f[:, c % 2, :])
                    nc.scalar.activation(out, s1[:, :, 0:HALF], ACT.Identity, bias=b_qk[:, i, c:c + 1],
                                         scale=SCALE if i == 0 else 1.0).then_inc(qk_staged, 1)

                def upper(b, h, part):
                    s, j, r = h % 2, (h // 2) % 2, DK * (h % 2)
                    if part == 0:
                        act.wait_ge(qk_staged, b * (2 * PAIRS) + (2 * (h // 2) + 2))
                        act.wait_ge(scores_ready, b * STEPS + (1 + (TILES * (h - 1) if h else 0)))
                        nc.scalar.activation(q_hi2[0:DK, s, 0:S], q_f[r:r + DK, j], ACT.Copy)
                        nc.scalar.activation(k_hilo[0:DK, s], k_f[r:r + DK, j], ACT.Copy).then_inc(head_hi, 1)
                    else:
                        nc.scalar.activation(q_hi2[DK:P, s, 0:S], q_f[r:r + DK, j], ACT.Copy)
                        if r:
                            nc.scalar.activation(k_hilo[DK:P, s], k_f[r:r + DK, j], ACT.Copy)
                        nc.scalar.activation(k_hi1[0:DK, s], k_f[r:r + DK, j], ACT.Copy).then_inc(hi_copied, 1)

                def exponentials(b, h, t):
                    act.wait_ge(biased, b * STEPS + (TILES * h + t + 2))
                    a = probs[0:tile_rows(t), (TILES * h + t) % 3, :]
                    nc.scalar.activation(a, a, ACT.Exp).then_inc(exped, 1)

                def take_context(b, h):
                    act.wait_ge(pv_done, b * STEPS + (TILES * (h + 1) + 1))
                    act.wait_ge(ctx_stored[h % 2], b * (PAIRS * 32) + (h // 2 * 32 + 1))
                    nc.scalar.activation(halves(ctx_sb[:, h % 2, S - 1::-1]), ct[:, :, 0:HALF],
                                         ACT.Copy).then_inc(ctx_copied, 1)

                def store_context(b, h):
                    r = DK * (h % 2)
                    act.wait_ge(ctx_copied, b * NH + (h + 2))
                    act.dma_start(dram["ctx"][h * DK:(h + 1) * DK, bass.ds(b * S, S)], ctx_sb[r:r + DK, h % 2, :])\
                       .then_inc(ctx_stored[h % 2], 16)
                    act.dma_start(dram["sums"][h:h + 1, bass.ds(b * S, S)], ctx_sb[DK - r:DK - r + 1, h % 2, :])\
                       .then_inc(ctx_stored[h % 2], 16)

                act.wait_ge(constants_set, 1)
                act.wait_ge(small_landed, 48)
                nc.scalar.mul(b_qk[:, 0], b_qk[:, 0], SCALE).then_inc(small_landed, 1)
                act.wait_ge(small_landed, 49)
                with act.Fori(0, images) as b:
                    stage(b, 0, 0)
                    stage(b, 1, 0)
                    upper(b, 0, 0)
                    upper(b, 0, 1)
                    for h in range(NH):
                        c = stages_pair(h)
                        if h + 1 < NH:
                            upper(b, h + 1, 0)
                        for t in range(TILES):
                            exponentials(b, h, t)
                            if t == 0 and c is not None:
                                stage(b, 0, c)
                            if t == 0 and h:
                                take_context(b, h - 1)
                            if t == 1 and c is not None:
                                stage(b, 1, c)
                            if t == 1 and h:
                                store_context(b, h - 1)
                            if t == 2 and h + 1 < NH:
                                upper(b, h + 1, 1)
                    take_context(b, NH - 1)
                    store_context(b, NH - 1)
                for stored in ctx_stored:
                    act.wait_ge(stored, images * PAIRS * 32 + 1)

            @block.vector
            def _(dve):
                def take_v(b, t):
                    dve.wait_ge(v_ready, b * TILES + (t + 2))
                    m = tile_rows(t)
                    src = st[t // 2 % 2][0:m, t % 2, :].rearrange("p (c e n) -> p c e n", e=2, n=DK)
                    nc.vector.tensor_tensor(v[0:m, t, :, 0:3:2, :], src,
                                            bv[0:m, :].rearrange("p (c e n) -> p c e n", e=2, n=DK),
                                            ALU.add).then_inc(v_staged, 1)

                def first_max(b, h, t):
                    dve.wait_ge(first_ready, b * STEPS + (TILES * h + t + 1))
                    dve.sem_inc(first_seen, 1)
                    top = (SHIFTS - ROWS + 1 - ROWS * t) * GRID + GRID - 1
                    nc.vector.tensor_tensor_reduce(s1[0:TILE, :, 0:HALF], s1[0:TILE, :, 0:HALF], window(h, TILE, top),
                                                   1.0, -3e38, ALU.add, ALU.max, maxima[:, t:t + 1]).then_inc(maxed, 1)

                def spread_max(b, h):
                    dve.wait_ge(turned, b * NH + (h + 1))
                    a = s1[0:TILES, 0:1, 0:TILE].to_broadcast([TILES, TILES, TILE])
                    nc.vector.tensor_tensor(q_lom[DK:DK + TILES, h % 2, :].rearrange("p (a n) -> p a n", a=TILES),
                                            a, spread[:, :, :], ALU.mult).then_inc(max_spread, 1)

                def add_bias(b, h, t):
                    s = TILES * h + t
                    dve.wait_ge(scores_ready, b * STEPS + (s + 2))
                    dve.wait_ge(pv_done, b * STEPS + (1 + (s - 2 if s >= 3 else 0)))
                    m = tile_rows(t)
                    top = ROWS * (TILES - 1 - t) * GRID + S - 1
                    nc.vector.tensor_tensor(halves(probs[0:m, s % 3, :]), st[s % 2][0:m, :, 0:HALF], window(h, m, top),
                                            ALU.add).then_inc(biased, 1)

                dve.wait_ge(constants_set, 1)
                dve.wait_ge(small_landed, 48)
                with dve.Fori(0, images) as b:
                    dve.wait_ge(pv_done, b * STEPS + 1)
                    for t in range(TILES):
                        for i in FIRST_V[t]:
                            first_max(b, 0, i)
                        if t == TURN_V:
                            spread_max(b, 0)
                        take_v(b, t)
                    for h in range(NH):
                        for t in range(TILES):
                            before, after, between = FIRST[stages_pair(h) is not None][t] if h + 1 < NH else (N, N, N)
                            if t == TILES - 1 and h + 1 < NH:
                                spread_max(b, h + 1)
                            if before is not N:
                                first_max(b, h + 1, before)
                            add_bias(b, h, t)
                            for i in (after, between):
                                if i is not N:
                                    first_max(b, h + 1, i)

            @block.tensor
            def _(pe):
                def project(b, i, c):
                    if i == 0:
                        pe.wait_ge(wqk_landed, (b * PAIRS + (c + 1)) * 16)
                        pe.wait_ge(max_spread, b * NH + (1 + (2 * c - 1 if c else 0)))
                    else:
                        pe.wait_ge(qk_staged, b * (2 * PAIRS) + (2 * c + 1))
                    for k in range(KC):
                        for w, xs in ((0, x_hi), (0, x_lo), (1, x_hi)):
                            for n in range(2):
                                mm = nc.tensor.matmul(s1[:, n, 0:HALF], w_qk[:, i, w, k, :],
                                                      xs[:, k, n * HALF:(n + 1) * HALF],
                                                      start=(k == 0 and w == 0 and xs is x_hi),
                                                      stop=(k == KC - 1 and w == 1))
                    mm.then_inc(qk_ready, 1)

                def project_v(b, t, between):
                    m = tile_rows(t)
                    if t < 4:
                        pe.wait_ge(biased, b * STEPS + 1)
                    else:
                        pe.wait_ge(v_staged, b * TILES + (t - 3))
                    for k in range(KC):
                        for xs, w in ((x_hi, wv_hi), (x_hi, wv_lo), (x_lo, wv_hi)):
                            mm = nc.tensor.matmul(st[t // 2 % 2][0:m, t % 2, :], xs[:, k, t * TILE:t * TILE + m], w[:, k, :],
                                                  start=(k == 0 and xs is x_hi and w is wv_hi),
                                                  stop=(k == KC - 1 and xs is x_lo))
                        if k == KC // 2 - 1 and between:
                            first_scores(b, 0, between[0])
                    mm.then_inc(v_ready, 1)
                    for i in between[1:]:
                        first_scores(b, 0, i)

                def first_scores(b, h, t):
                    s = h % 2
                    if t == 0:
                        pe.wait_ge(head_hi, b * NH + (h + 1))
                        pe.wait_ge(qk_staged, b * (2 * PAIRS) + 2 * min(PAIRS, (h + 1) // 2 + 1 if h else 1))
                        if h:
                            pe.wait_ge(max_spread, b * NH + (h + 1))
                    else:
                        pe.wait_ge(maxed, b * STEPS + (TILES * h + t))
                    for n in range(2):
                        mm = nc.tensor.matmul(s1[0:TILE, n, 0:HALF], q_hi2[0:DK, s, t * TILE:(t + 1) * TILE],
                                              k_hilo[0:DK, s, n * HALF:(n + 1) * HALF], start=True, stop=True)
                    mm.then_inc(first_ready, 1)

                def turn_max(b, h):
                    pe.wait_ge(maxed, b * STEPS + TILES * (h + 1))
                    nc.tensor.matmul(s1[0:TILES, 0, 0:TILE], maxima[:, :], ident[:, :], start=True, stop=True)\
                      .then_inc(turned, 1)

                def scores(b, h, t):
                    s, m, i = h % 2, tile_rows(t), TILES * h + t
                    if t == 0:
                        pe.wait_ge(lo_split, b * NH + (h + 2))
                        pe.wait_ge(max_spread, b * NH + (h + 2))
                    if i < 2:
                        pe.wait_ge(v_staged, b * TILES + TILES)
                    else:
                        pe.wait_ge(biased, b * STEPS + (i - 1 + 1))
                    for n in range(2):
                        q = slice(n * HALF, (n + 1) * HALF)
                        nc.tensor.matmul(st[i % 2][0:m, n, 0:HALF], k_hilo[:, s, t * TILE:t * TILE + m], q_hi2[:, s, q],
                                         start=True, stop=False)
                    for n in range(2):
                        q = slice(n * HALF, (n + 1) * HALF)
                        mm = nc.tensor.matmul(st[i % 2][0:m, n, 0:HALF], k_hi1[:, s, t * TILE:t * TILE + m], q_lom[:, s, q],
                                              start=False, stop=True)
                    mm.then_inc(scores_ready, 1)

                def weigh_values(b, h, t, h_next=None, between=None):
                    m, i = tile_rows(t), TILES * h + t
                    pe.wait_ge(exped, b * STEPS + (i + 1))
                    if t == 0:
                        pe.wait_ge(ctx_copied, b * NH + (h + 1))
                    e = h % 2
                    vs = v[0:m, t, h // 2, e:e + 2, :].rearrange("p a n -> p (a n)")
                    for n in range(2):
                        mm = nc.tensor.matmul(ct[:, n, 0:HALF], vs, probs[0:m, i % 3, n * HALF:(n + 1) * HALF],
                                              start=(t == 0), stop=(t == TILES - 1))
                        if n == 0 and between is not N:
                            first_scores(b, h_next, between)
                    mm.then_inc(pv_done, 1)

                pe.wait_ge(constants_set, 1)
                with pe.Fori(0, images) as b:
                    pe.wait_ge(x_split, b * KC + (KC + 1))
                    project(b, 0, 0)
                    project(b, 1, 0)
                    for t in range(TILES):
                        if t == TURN_V:
                            turn_max(b, 0)
                        project_v(b, t, FIRST_V[t])
                    late = []
                    for h in range(NH):
                        c = stages_pair(h)
                        for t in range(TILES):
                            before, after, between = FIRST[c is not None][t] if h + 1 < NH else (N, N, N)
                            if t == TILES - 1 and h + 1 < NH:
                                turn_max(b, h + 1)
                            if before is not N:
                                first_scores(b, h + 1, before)
                            scores(b, h, t)
                            late.append((h, t))
                            if t == 0 and c is not None:
                                project(b, 0, c)
                            if after is not N:
                                first_scores(b, h + 1, after)
                            for u in range(2 if t == TILES - 1 else 1 if t and len(late) > PV_LAG else 0):
                                weigh_values(b, *late.pop(0), h + 1, between if not u else N)
                            if t == 1 and c is not None:
                                project(b, 1, c)
                    for at in late:
                        weigh_values(b, *at)


TOKENS = IMAGES * S
SUB = 120
SUBS = 3
TT = SUB * SUBS
NT = TOKENS // TT
NEWTON = 3
RSQRT_MAGIC = 0x5F3759DF


def feed_forward(nc, dram):
    with ExitStack() as ctx:
        def sb(name, shape, dt=F32):
            return ctx.enter_context(nc.sbuf_tensor(name, shape, dt))

        def ps(name, shape):
            return ctx.enter_context(nc.psum_tensor(name, shape, F32))

        def sem(name):
            return ctx.enter_context(nc.semaphore(name))

        wo = [sb(f"wo_{p}", [P, KC, D], F32R) for p in ("hi", "lo")]
        w1 = [sb(f"w1_{p}", [P, KC, FF], F32R) for p in ("hi", "lo")]
        w2 = [sb(f"w2_{p}", [P, FC, D], F32R) for p in ("hi", "lo")]
        bo_row, g1_row, be1_row, g2_row, be2_row = (sb(n, [SUB, D]) for n in ("bo_row", "g1_row", "be1_row", "g2_row", "be2_row"))
        b1_col = sb("b1_col", [P, FC])
        g1_col = sb("g1_col", [P, KC])
        be1_col = sb("be1_col", [P, KC])
        ident = sb("ident2", [SUB, SUB])
        y_ps = ps("y_ps", [P, SUBS, 512])
        h_ps = ps("h_ps", [P, 2, 512])
        z_ps = ps("z_ps", [P, SUBS, 512])

        weights_landed = [sem("weights_landed0"), sem("weights_landed1")]
        weights_hi = sem("weights_hi")
        weights_lo = sem("weights_lo")
        rows_landed = sem("rows_landed")
        b2_landed = sem("b2_landed")
        rows_added = sem("rows_added")
        sums_landed = sem("sums_landed")
        inverted = sem("inverted")
        inverse_stored = sem("inverse_stored")
        ident_set = sem("ident_set")

        with ExitStack() as early:
            raw = early.enter_context(nc.sbuf_tensor("raw2", [P, 2, FF], F32))
            sums = early.enter_context(nc.sbuf_tensor("sums_sb", [P, NH * TOKENS // P], F32))
            b2_row = early.enter_context(nc.sbuf_tensor("b2_row", [SUB, D], F32))
            parts = [(dram["w_o"].rearrange("(k p) n -> p k n", p=P), wo, slice(0, KC))]
            parts += [(dram["w1"][k * P:(k + 1) * P, :], w1, k) for k in range(KC)]
            w2_view = dram["w2"].rearrange("(f p) n -> p f n", p=P)
            parts += [(w2_view[:, 4 * j:4 * j + 4, :], w2, slice(4 * j, 4 * j + 4)) for j in range(4)]

            def raw_view(n, at):
                a = raw[:, n % 2, :]
                return a if isinstance(at, int) else a.rearrange("p (k n) -> p k n", n=D)

            with nc.Block() as block:
                @block.sync
                def _(sp):
                    sp.dma_start(sums[:, :], dram["sums"].rearrange("h (a n) -> (h a) n", a=P // NH)).then_inc(sums_landed, 16)
                    for row, name in ((bo_row, "b_o"), (g1_row, "ln1_g"), (be1_row, "ln1_b"), (g2_row, "ln2_g"),
                                      (be2_row, "ln2_b"), (b2_row, "b2")):
                        sp.dma_start(row[:, :], dram[name].to_broadcast([SUB, D])).then_inc(rows_landed, 16)
                    for col, name in ((b1_col, "b1"), (g1_col, "ln1_g_col"), (be1_col, "ln1_b_col")):
                        sp.dma_start(col[:, :], dram[name]).then_inc(rows_landed, 16)
                    for n, (src, _, at) in enumerate(parts):
                        if n >= 2:
                            sp.wait_ge(weights_lo, n - 1)
                        sp.dma_start(raw_view(n, at), src).then_inc(weights_landed[n % 2], 16)
                    sp.wait_ge(inverted, 1)
                    sp.dma_start(dram["inverse"].rearrange("h (a n) -> (h a) n", a=P // NH), sums[:, :])\
                      .then_inc(inverse_stored, 16)
                    sp.wait_ge(inverse_stored, 16)
                    sp.wait_ge(rows_landed, 16 * 9)

                @block.scalar
                def _(act):
                    for n, (_, to, at) in enumerate(parts):
                        act.wait_ge(weights_landed[n % 2], 16 * (n // 2 + 1))
                        nc.scalar.activation(to[0][:, at], raw_view(n, at), ACT.Copy).then_inc(weights_hi, 1)

                @block.vector
                def _(dve):
                    dve.wait_ge(sums_landed, 16)
                    nc.vector.reciprocal(sums[:, :], sums[:, :]).then_inc(inverted, 1)
                    for n, (_, to, at) in enumerate(parts):
                        dve.wait_ge(weights_hi, n + 1)
                        nc.vector.tensor_tensor(to[1][:, at], raw_view(n, at), to[0][:, at].bitcast(F32),
                                                ALU.subtract).then_inc(weights_lo, 1)

                @block.gpsimd
                def _(pool):
                    nc.gpsimd.memset(ident[:, :], 0.0).then_inc(ident_set, 1)
                    pool.wait_ge(ident_set, 1)
                    nc.gpsimd.affine_select(out=ident[:, :], in_=ident[:, :], compare_op=ALU.not_equal, fill=1.0,
                                            base=0, pattern=[[-1, SUB]], channel_multiplier=1).then_inc(ident_set, 1)
                    pool.wait_ge(rows_landed, 16 * 9)
                    nc.gpsimd.tensor_tensor(be1_row[:, :], be1_row[:, :], b2_row[:, :], ALU.add).then_inc(rows_added, 1)

        c_raw = sb("c_raw", [P, 2, TT])
        c_inv = sb("c_inv", [P, 2, TT])
        res = sb("res", [SUB, 2, SUBS, D])
        parts_t = [[sb(f"parts_{p}_{e}", [P, KC, TT], F32R) for p in ("hi", "lo")] for e in range(2)]
        g = sb("g", [P, 2, TT])
        h_t = [sb(f"h_{p}", [P, 2, TT], F32R) for p in ("hi", "lo")]
        stats = sb("stats", [SUB, 6])
        mean_var = sb("mean_var", [SUB, SUBS, 2])
        var = sb("var", [SUB, SUBS])
        root = sb("root", [SUB, SUBS])
        step = sb("step", [SUB, SUBS])

        ctx_landed = [sem("ctx_landed0"), sem("ctx_landed1")]
        sp_passed = sem("sp_passed")
        divided = sem("divided")
        ctx_hi = sem("ctx_hi")
        ctx_split = sem("ctx_split")
        x_landed = [sem("x_landed_even"), sem("x_landed_odd")]
        x_biased = sem("x_biased")
        z_ready = sem("z_ready")
        z_taken = sem("z_taken")
        ln_step = sem("ln_step")
        ln_passed = sem("ln_passed")
        normed1 = sem("normed1")
        normed2 = sem("normed2")
        turned = sem("turned2")
        turn_staged = sem("turn_staged")
        a_hi = sem("a_hi")
        a_split = sem("a_split")
        h_ready = sem("h_ready")
        g_done = sem("g_done")
        h_hi = sem("h_hi")
        h_split = sem("h_split")
        y_step = sem("y_step")
        y_taken = sem("y_taken")
        scaled = sem("scaled")
        residual_ready = sem("residual_ready")
        out_ready = sem("out_ready")
        out_stored = [sem("out_stored_even"), sem("out_stored_odd")]
        LN_OPS = SUBS * 2 + 3 + 3 * NEWTON
        CONTEXT_AT, OUT_AT, NORM_AT, TURN_AT = 2, 6, 8, 13
        TURNED = [[]] * TURN_AT + [[0, 1, 2], [3]] + [[]] * (FC - TURN_AT - 2)
        TAKEN = [[]] * TURN_AT + [[0, 1], [2, 3]] + [[]] * (FC - TURN_AT - 2)

        def tiles(eng, front, body, tail):
            front(0, 0, 0)
            body(0, 0, 0, False, True)
            with eng.Fori(0, (NT - 2) // 2) as u:
                body(u * 2 + 1, u, 1, True, True)
                body(u * 2 + 2, u + 1, 0, True, True)
            body(NT - 1, (NT - 1) // 2, 1, True, False)
            tail(NT - 1, 1)

        def nothing(*_):
            return None

        with nc.Block() as block:
            @block.sync
            def _(sp):
                def load_context(t):
                    sp.wait_ge(a_split, t * KC)
                    for c in range(KC):
                        sp.wait_ge(ctx_split, t * KC + (c - 1 if c >= 2 else 0))
                        sp.sem_inc(sp_passed, 1)
                        sp.dma_start(c_raw[:, c % 2], dram["ctx"][c * P:(c + 1) * P, bass.ds(t * TT, TT)])\
                          .then_inc(ctx_landed[c % 2], 16)
                        for i in range(2):
                            sp.dma_start(c_inv[i * DK:(i + 1) * DK, c % 2],
                                         dram["inverse"][2 * c + i:2 * c + i + 1, bass.ds(t * TT, TT)].to_broadcast([DK, TT]))\
                              .then_inc(ctx_landed[c % 2], 16)

                def load_x(t, u, e):
                    sp.wait_ge(out_stored[e], u * 16)
                    sp.dma_start(res[:, e], dram["x"][bass.ds(t * TT, TT), :].rearrange("(s p) n -> p s n", p=SUB))\
                      .then_inc(x_landed[e], 16)

                def front(t, u, e):
                    load_context(t)
                    load_x(t, u, e)

                def store(t, e):
                    sp.wait_ge(out_ready, t + 1)
                    sp.dma_start(dram["out"][bass.ds(t * TT, TT), :].rearrange("(s p) n -> p s n", p=SUB), res[:, e])\
                      .then_inc(out_stored[e], 16)

                def body(t, u, e, has_prev, has_next):
                    if has_next:
                        load_context(t + 1)
                    if has_prev:
                        store(t - 1, 1 - e)
                    if has_next:
                        load_x(t + 1, u + e, 1 - e)

                tiles(sp, front, body, store)
                sp.wait_ge(out_stored[0], NT // 2 * 16)
                sp.wait_ge(out_stored[1], NT // 2 * 16)

            @block.gpsimd
            def _(pool):
                def divide_context(t, e):
                    for c in range(KC):
                        pool.wait_ge(ctx_landed[c % 2], (t * 2 + (c // 2 + 1)) * 48)
                        nc.gpsimd.tensor_tensor(c_raw[:, c % 2], c_raw[:, c % 2], c_inv[:, c % 2], ALU.mult).then_inc(divided, 1)
                        pool.wait_ge(ctx_hi, t * KC + (c + 1))
                        nc.gpsimd.tensor_tensor(parts_t[e][1][:, c], c_raw[:, c % 2], parts_t[e][0][:, c].bitcast(F32),
                                                ALU.subtract).then_inc(ctx_split, 1)

                def bias_x(u, e):
                    pool.wait_ge(x_landed[e], (u + 1) * 16)
                    for s in range(SUBS):
                        nc.gpsimd.tensor_tensor(res[:, e, s], res[:, e, s], bo_row[:, :], ALU.add).then_inc(x_biased, 1)

                def scale_and_shift(n, e, g_row, b_row, done):
                    for s in range(SUBS):
                        nc.gpsimd.tensor_tensor(res[:, e, s], res[:, e, s], g_row[:, :], ALU.mult).then_inc(scaled, 1)
                    pool.wait_ge(scaled, n * SUBS + SUBS)
                    for s in range(SUBS):
                        i = nc.gpsimd.tensor_tensor(res[:, e, s], res[:, e, s], b_row[:, :], ALU.add)
                    i.then_inc(done, 1)

                def body(t, u, e, has_prev, has_next):
                    if has_next:
                        divide_context(t + 1, 1 - e)
                    if has_prev:
                        pool.wait_ge(normed2, t * SUBS)
                        scale_and_shift(t * 2, 1 - e, g2_row, be2_row, out_ready)
                    if has_next:
                        bias_x(u + e, 1 - e)
                        pool.wait_ge(turned, t * KC + 2 * KC)
                        scale_and_shift(t * 2 + 1, 1 - e, g1_row, be1_row, residual_ready)

                def first(t, u, e):
                    divide_context(t, e)
                    bias_x(u, e)
                    pool.wait_ge(turned, KC)
                    scale_and_shift(0, e, g1_row, be1_row, residual_ready)

                def tail(t, e):
                    pool.wait_ge(normed2, NT * SUBS)
                    scale_and_shift(2 * NT - 1, e, g2_row, be2_row, out_ready)

                tiles(pool, first, body, tail)

            @block.scalar
            def _(act):
                def context_upper(t, e, c):
                    act.wait_ge(divided, t * KC + (c + 1))
                    nc.scalar.activation(parts_t[e][0][:, c], c_raw[:, c % 2], ACT.Copy).then_inc(ctx_hi, 1)

                def take_turned(t, e, c):
                    act.wait_ge(turned, t * KC + (c + 1))
                    if c < 2:
                        act.wait_ge(ctx_split, t * KC + KC)
                    else:
                        act.wait_ge(a_split, t * KC + (c - 1))
                    nc.scalar.activation(c_raw[:, c % 2], z_ps[:, c % SUBS, 0:TT], ACT.Identity, bias=be1_col[:, c:c + 1],
                                         scale=g1_col[:, c:c + 1]).then_inc(turn_staged, 1)
                    act.wait_ge(turn_staged, t * KC + (c + 1))
                    nc.scalar.activation(parts_t[e][0][:, c], c_raw[:, c % 2], ACT.Copy).then_inc(a_hi, 1)

                def gelu(t, f):
                    act.wait_ge(h_ready, t * FC + (f + 1))
                    act.wait_ge(h_split, t * FC + (f - 1 if f >= 2 else 0))
                    nc.scalar.activation(g[:, f % 2], h_ps[:, f % 2, 0:TT], ACT.Gelu, bias=b1_col[:, f:f + 1])\
                      .then_inc(g_done, 1)
                    act.wait_ge(y_step, t * FC + (f - 1 if f >= 2 else 0))
                    act.wait_ge(g_done, t * FC + (f + 1))
                    nc.scalar.activation(h_t[0][:, f % 2], g[:, f % 2], ACT.Copy).then_inc(h_hi, 1)

                def front(t, u, e):
                    for c in range(KC):
                        context_upper(t, e, c)
                    for c in range(KC):
                        take_turned(t, e, c)

                def body(t, u, e, has_prev, has_next):
                    for f in range(FC):
                        gelu(t, f)
                        if CONTEXT_AT <= f < CONTEXT_AT + KC and has_next:
                            context_upper(t + 1, 1 - e, f - CONTEXT_AT)
                        for c in TAKEN[f] if has_next else ():
                            take_turned(t + 1, 1 - e, c)

                tiles(act, front, body, nothing)

            @block.vector
            def _(dve):
                def then(i, q, n):
                    i.then_inc(ln_step, 1)
                    dve.wait_ge(ln_step, q * LN_OPS + n)

                def moments(q, e, s):
                    then(nc.vector.bn_stats(stats[:, :], res[:, e, s]), q, 2 * s + 1)
                    dve.sem_inc(ln_passed, 1)
                    then(nc.vector.bn_aggr(mean_var[:, s, :], stats[:, :]), q, 2 * s + 2)

                def inverse_roots(q):
                    n = 2 * SUBS
                    bits = root[:, :].bitcast(I32)
                    then(nc.vector.tensor_scalar(var[:, :], mean_var[:, :, 1], LN_EPS, None, ALU.add), q, n + 1)
                    then(nc.vector.tensor_scalar(bits, var[:, :].bitcast(I32), 1, None, ALU.logical_shift_right), q, n + 2)
                    then(nc.vector.tensor_scalar(bits, bits, -1.0, float(RSQRT_MAGIC), ALU.mult, ALU.add), q, n + 3)
                    n += 3
                    for _ in range(NEWTON):
                        then(nc.vector.tensor_tensor(step[:, :], root[:, :], root[:, :], ALU.mult), q, n + 1)
                        then(nc.vector.scalar_tensor_tensor(out=step[:, :], in0=step[:, :], scalar=-0.5, in1=var[:, :],
                                                            op0=ALU.mult, op1=ALU.mult), q, n + 2)
                        then(nc.vector.scalar_tensor_tensor(out=root[:, :], in0=step[:, :], scalar=1.5, in1=root[:, :],
                                                            op0=ALU.add, op1=ALU.mult), q, n + 3)
                        n += 3

                def normalise(e, done):
                    for s in range(SUBS):
                        nc.vector.tensor_scalar(res[:, e, s], res[:, e, s], mean_var[:, s, 0:1], root[:, s:s + 1],
                                                ALU.subtract, ALU.mult).then_inc(done, 1)

                def take_z(t, e, s):
                    dve.wait_ge(x_biased, t * SUBS + (s + 1))
                    dve.wait_ge(z_ready, t * SUBS + (s + 1))
                    nc.vector.tensor_tensor(res[:, e, s], z_ps[0:SUB, s, :], res[:, e, s], ALU.add).then_inc(z_taken, 1)
                    dve.wait_ge(z_taken, t * SUBS + (s + 1))

                def a_lower(t, e, c):
                    dve.wait_ge(a_hi, t * KC + (c + 1))
                    nc.vector.tensor_tensor(parts_t[e][1][:, c], c_raw[:, c % 2], parts_t[e][0][:, c].bitcast(F32),
                                            ALU.subtract).then_inc(a_split, 1)

                def h_lower(t, f):
                    dve.wait_ge(h_hi, t * FC + (f + 1))
                    nc.vector.tensor_tensor(h_t[1][:, f % 2], g[:, f % 2], h_t[0][:, f % 2].bitcast(F32),
                                            ALU.subtract).then_inc(h_split, 1)

                def take_y(t, e):
                    dve.wait_ge(residual_ready, t + 1)
                    dve.wait_ge(y_step, t * FC + FC)
                    for s in range(SUBS):
                        nc.vector.tensor_tensor(res[:, e, s], y_ps[0:SUB, s, :], res[:, e, s], ALU.add).then_inc(y_taken, 1)

                def front(t, u, e):
                    for s in range(SUBS):
                        take_z(0, 0, s)
                        moments(0, 0, s)
                    inverse_roots(0)
                    normalise(0, normed1)
                    for c in range(KC):
                        a_lower(0, 0, c)

                def body(t, u, e, has_prev, has_next):
                    for f in range(FC):
                        h_lower(t, f)
                        if has_prev:
                            if f == 0:
                                dve.wait_ge(y_taken, t * SUBS)
                            if f < SUBS:
                                moments(t * 2, 1 - e, f)
                            if f == SUBS:
                                inverse_roots(t * 2)
                                normalise(1 - e, normed2)
                        if has_next:
                            if NORM_AT <= f < NORM_AT + SUBS:
                                take_z(t + 1, 1 - e, f - NORM_AT)
                                moments(t * 2 + 1, 1 - e, f - NORM_AT)
                            if f == NORM_AT + SUBS:
                                inverse_roots(t * 2 + 1)
                                normalise(1 - e, normed1)
                            for c in TAKEN[f]:
                                a_lower(t + 1, 1 - e, c)
                    take_y(t, e)

                def tail(t, e):
                    dve.wait_ge(y_taken, NT * SUBS)
                    for s in range(SUBS):
                        moments(NT * 2 - 1, e, s)
                    inverse_roots(NT * 2 - 1)
                    normalise(e, normed2)

                tiles(dve, front, body, tail)

            @block.tensor
            def _(pe):
                PASSES = ((0, 0), (0, 1), (1, 0))

                def project_out(t, e, s):
                    if s == 0:
                        pe.wait_ge(ctx_split, t * KC + KC)
                        pe.wait_ge(turn_staged, t * KC)
                    for k in range(KC):
                        for x, w in PASSES:
                            mm = nc.tensor.matmul(z_ps[0:SUB, s, :], parts_t[e][x][:, k, s * SUB:(s + 1) * SUB], wo[w][:, k, :],
                                                  start=(k + x + w == 0), stop=(k == KC - 1 and x == 1))
                    mm.then_inc(z_ready, 1)

                def turn(t, e, c):
                    if c == 0:
                        pe.wait_ge(normed1, t * SUBS + SUBS)
                    if c >= SUBS:
                        pe.wait_ge(turn_staged, t * KC + (c - SUBS + 1))
                    for s in range(SUBS):
                        mm = nc.tensor.transpose(z_ps[:, c % SUBS, s * SUB:(s + 1) * SUB], res[:, e, s, c * P:(c + 1) * P],
                                                 ident[:, :])
                    mm.then_inc(turned, 1)

                def widen(t, e, f):
                    if f == 0:
                        pe.wait_ge(a_split, t * KC + KC)
                    pe.wait_ge(g_done, t * FC + (f - 1 if f >= 2 else 0))
                    for k in range(KC):
                        for x, w in ((0, 0), (1, 0), (0, 1)):
                            mm = nc.tensor.matmul(h_ps[:, f % 2, 0:TT], w1[w][:, k, f * P:(f + 1) * P], parts_t[e][x][:, k, :],
                                                  start=(k + x + w == 0), stop=(k == KC - 1 and w == 1))
                    mm.then_inc(h_ready, 1)

                def narrow(t, f):
                    pe.wait_ge(h_split, t * FC + (f + 1))
                    if f == 0:
                        pe.wait_ge(y_taken, t * SUBS)
                    for s in range(SUBS):
                        for x, w in PASSES:
                            mm = nc.tensor.matmul(y_ps[0:SUB, s, :], h_t[x][:, f % 2, s * SUB:(s + 1) * SUB], w2[w][:, f, :],
                                                  start=(f + x + w == 0), stop=(f == FC - 1 and x == 1))
                    mm.then_inc(y_step, 1)

                def front(t, u, e):
                    for s in range(SUBS):
                        project_out(0, 0, s)
                    for c in range(KC):
                        turn(0, 0, c)

                def body(t, u, e, has_prev, has_next):
                    for f in range(FC):
                        widen(t, e, f)
                        for c in TURNED[f] if has_next else ():
                            turn(t + 1, 1 - e, c)
                        if f:
                            narrow(t, f - 1)
                        if OUT_AT <= f < OUT_AT + SUBS and has_next:
                            project_out(t + 1, 1 - e, f - OUT_AT)
                    narrow(t, FC - 1)

                tiles(pe, front, body, nothing)


def build(nc, dram, images=IMAGES):
    with ExitStack() as ctx:
        bias = ctx.enter_context(nc.sbuf_tensor("bias", [TILE, NH, WINDOW], F32))
        wv_hi = ctx.enter_context(nc.sbuf_tensor("wv_hi", [P, KC, D], F32R))
        wv_lo = ctx.enter_context(nc.sbuf_tensor("wv_lo", [P, KC, D], F32R))
        prepare_tables(nc, dram, bias, wv_hi, wv_lo)
        attention(nc, dram, bias, wv_hi, wv_lo, images)
    feed_forward(nc, dram)


def displacement_onehot():
    import numpy as np

    r, c = np.indices((UROWS, UCOLS))
    dh = (GRID + 1 - r).astype(np.float64)
    dw = (GRID - 1 - c).astype(np.float64)
    dist = np.minimum(np.sqrt(dh ** 2 + dw ** 2).astype(np.int64), DISTS - 1)
    direction = ((np.arctan2(dh, dw) + np.pi) / (2.0 * np.pi) * DIRS).astype(np.int64) % DIRS
    direction = np.where((dh == 0) & (dw == 0), 0, direction)
    out = np.zeros((DISTS + DIRS, r.size), np.float32)
    out[dist.ravel(), np.arange(r.size)] = 1.0
    out[DISTS + direction.ravel(), np.arange(r.size)] = 1.0
    return out


def kernel(**inputs):
    import numpy as np
    import concourse.bacc as bacc
    from concourse.bass_utils import run_bass_kernel_spmd

    def given(name):
        return np.ascontiguousarray(inputs[name if name == "x" else "L0_conv_" + name])

    def columns(name):
        return np.ascontiguousarray(given(name).reshape(-1, P).T)

    x = given("x").reshape(TOKENS, D)
    arrays = {"x": x, "x_t": np.ascontiguousarray(x.T), "displacement_onehot": displacement_onehot()}
    for name in ("dist_bias", "dir_bias", "w_q", "w_k", "w_v", "w_o", "w1", "w2"):
        arrays[name] = given(name)
    for name in ("b_q", "b_k", "b1"):
        arrays[name] = columns(name)
    for name in ("b_v", "b_o", "b2", "ln1_g", "ln1_b", "ln2_g", "ln2_b"):
        arrays[name] = given(name).reshape(1, D)
    for name in ("ln1_g", "ln1_b"):
        arrays[name + "_col"] = columns(name)

    nc = bacc.Bacc("TRN2", target_bir_lowering=False, num_devices=1)
    dram = {name: nc.dram_tensor(name, a.shape, mybir.dt.from_np(a.dtype), kind="ExternalInput").ap()
            for name, a in arrays.items()}
    for name, shape in (("skew", (NH, GRID, UROWS * GRID)), ("qk_weights", (PAIRS, P, 4 * KC * P)),
                        ("ctx", (D, TOKENS)), ("sums", (NH, TOKENS)), ("inverse", (NH, TOKENS))):
        dram[name] = nc.dram_tensor(name, shape, F32, kind="Internal").ap()
    dram["out"] = nc.dram_tensor("out", (TOKENS, D), F32, kind="ExternalOutput").ap()
    build(nc, dram)
    got = run_bass_kernel_spmd(nc, [arrays], core_ids=[0])
    return got.results[0]["out"].reshape(IMAGES, GRID, GRID, D)
```

```python
from contextlib import ExitStack

import concourse.bass as bass
from concourse import mybir

F32 = mybir.dt.float32
F32R = mybir.dt.float32r
I32 = mybir.dt.int32
ALU = mybir.AluOpType
ACT = mybir.ActivationFunctionType

P = 128
IMAGES, GRID, D = 8, 30, 512
S = GRID * GRID
NH = 8
DK = D // NH
FF = 2048
KC = D // P
PAIRS = NH // 2
FC = FF // P
LN_EPS = 1e-5
DISTS, DIRS = 60, 16

ROWS = 4
TILE = ROWS * GRID
TILES = -(-GRID // ROWS)
LAST = S - (TILES - 1) * TILE
SPAD = TILES * TILE
HALF = S // 2
SHIFTS = GRID + ROWS * (TILES - 1) + 2
UROWS, UCOLS = SHIFTS + ROWS - 1, 2 * GRID - 1
WINDOW = SHIFTS * GRID
SCALE = DK ** -0.5


def tile_rows(t):
    return TILE if t < TILES - 1 else LAST


def prepare(nc, dram, x_hi, x_lo, wv, v, k_hi1, q_hi2, ident, spread):
    with ExitStack() as ctx:
        def sb(name, shape, dt=F32):
            return ctx.enter_context(nc.sbuf_tensor(name, shape, dt))

        def sem(name):
            return ctx.enter_context(nc.semaphore(name))

        CH = 413
        NCH = UROWS * UCOLS // CH
        assert NCH * CH == UROWS * UCOLS
        table = sb("table", [DISTS + DIRS, NH])
        onehot = sb("onehot", [DISTS + DIRS, UROWS * UCOLS])
        u_sb = sb("u_sb", [NH, UROWS * UCOLS])
        qk_split = sb("qk_split", [P, PAIRS, 2, 2, KC, P], F32R)
        u_ps = ctx.enter_context(nc.psum_tensor("u_ps", [P, 4, 512], F32))

        table_landed = sem("table_landed")
        raw_landed = [sem("wq_landed"), sem("wk_landed"), sem("wv_landed")]
        first_x_landed = sem("first_x_landed")
        u_ready = sem("u_ready")
        u_copied = sem("u_copied")
        skew_stored = sem("skew_stored")
        x_hi_done = sem("first_x_hi")
        w_hi_done = sem("w_hi_done")
        w_lo_done = sem("w_lo_done")
        split_stored = sem("split_stored")
        constant_step = sem("constant_step")
        u_view = u_sb[:, :].rearrange("h (r c) -> h r c", c=UCOLS)

        with nc.Block() as block:
            @block.sync
            def _(sp):
                sp.dma_start(table[0:DISTS, :], dram["dist_bias"]).then_inc(table_landed, 16)
                sp.dma_start(table[DISTS:DISTS + DIRS, :], dram["dir_bias"]).then_inc(table_landed, 16)
                sp.dma_start(onehot[:, :], dram["displacement_onehot"]).then_inc(table_landed, 16)
                for i, name in enumerate(("w_q", "w_k")):
                    for k in range(KC):
                        sp.dma_start(qk_split[:, :, i, 1, k].bitcast(F32),
                                     dram[name][k * P:(k + 1) * P, :].rearrange("p (c n) -> p c n", c=PAIRS))\
                          .then_inc(raw_landed[i], 16)
                with sp.Fori(0, KC) as k:
                    sp.dma_start(wv[:, 1, bass.ds(k, 1)].rearrange("p a n -> p (a n)").bitcast(F32),
                                 dram["w_v"][bass.ds(k * P, P), :]).then_inc(raw_landed[2], 16)
                with sp.Fori(0, KC) as k:
                    sp.dma_start(x_lo[:, bass.ds(k, 1)].rearrange("p a n -> p (a n)").bitcast(F32),
                                 dram["x_t"][bass.ds(k * P, P), 0:S]).then_inc(first_x_landed, 16)
                sp.wait_ge(u_copied, NCH)
                for w in range(GRID):
                    sp.dma_start(dram["skew"][:, w].rearrange("h (r c) -> h r c", c=GRID),
                                 u_view[:, :, GRID - 1 - w:2 * GRID - 1 - w]).then_inc(skew_stored, 16)
                sp.wait_ge(skew_stored, 16 * GRID)

            @block.scalar
            def _(act):
                for i in range(2):
                    act.wait_ge(raw_landed[i], 16 * KC)
                    for c in range(PAIRS):
                        nc.scalar.activation(qk_split[:, c, i, 0], qk_split[:, c, i, 1].bitcast(F32),
                                             ACT.Copy).then_inc(w_hi_done, 1)
                act.wait_ge(raw_landed[2], 16 * KC)
                nc.scalar.activation(wv[:, 0], wv[:, 1].bitcast(F32), ACT.Copy).then_inc(w_hi_done, 1)
                act.wait_ge(first_x_landed, 16 * KC)
                for k in range(KC):
                    nc.scalar.activation(x_hi[:, k], x_lo[:, k].bitcast(F32), ACT.Copy).then_inc(x_hi_done, 1)
                act.wait_ge(w_lo_done, 2 * PAIRS)
                act.dma_start(dram["qk_weights"].rearrange("c p n -> p c n"),
                              qk_split[:, :, :, :, :, :].rearrange("p c i s k n -> p c (i s k n)").bitcast(F32)).then_inc(split_stored, 16)
                act.wait_ge(split_stored, 16)

            @block.vector
            def _(dve):
                for j in range(NCH):
                    dve.wait_ge(u_ready, j + 1)
                    nc.vector.tensor_copy(u_sb[:, j * CH:(j + 1) * CH], u_ps[0:NH, j % 4, 0:CH]).then_inc(u_copied, 1)
                n = 0
                for i in range(2):
                    for c in range(PAIRS):
                        n += 1
                        dve.wait_ge(w_hi_done, n)
                        nc.vector.tensor_tensor(qk_split[:, c, i, 1], qk_split[:, c, i, 1].bitcast(F32),
                                                qk_split[:, c, i, 0].bitcast(F32), ALU.subtract).then_inc(w_lo_done, 1)
                dve.wait_ge(w_hi_done, n + 1)
                nc.vector.tensor_tensor(wv[:, 1], wv[:, 1].bitcast(F32), wv[:, 0].bitcast(F32),
                                        ALU.subtract).then_inc(w_lo_done, 1)
                for k in range(KC):
                    dve.wait_ge(x_hi_done, k + 1)
                    nc.vector.tensor_tensor(x_lo[:, k], x_lo[:, k].bitcast(F32), x_hi[:, k].bitcast(F32), ALU.subtract)

            @block.gpsimd
            def _(pool):
                nc.gpsimd.memset(ident[:, :], 0.0).then_inc(constant_step, 1)
                nc.gpsimd.memset(spread[:, :, :], -1.0).then_inc(constant_step, 1)
                pool.wait_ge(constant_step, 2)
                nc.gpsimd.affine_select(out=ident[:, :], in_=ident[:, :], compare_op=ALU.not_equal, fill=1.0,
                                        base=0, pattern=[[-1, TILE]], channel_multiplier=1).then_inc(constant_step, 1)
                flat = spread[:, :, :].rearrange("p a n -> p (a n)")
                nc.gpsimd.affine_select(out=flat, in_=flat, compare_op=ALU.is_ge, fill=0.0, base=0,
                                        pattern=[[1, SPAD]], channel_multiplier=-TILE).then_inc(constant_step, 1)
                pool.wait_ge(constant_step, 4)
                nc.gpsimd.affine_select(out=flat, in_=flat, compare_op=ALU.is_ge, fill=0.0, base=TILE - 1,
                                        pattern=[[-1, SPAD]], channel_multiplier=TILE)
                for t in range(TILES):
                    nc.gpsimd.memset(v[:, t, :, DK:DK + 1], 1.0)
                nc.gpsimd.memset(q_hi2[:, :, S:SPAD].bitcast(F32), 0.0).then_inc(constant_step, 1)
                pool.wait_ge(constant_step, 5)
                nc.gpsimd.memset(k_hi1[DK:DK + TILES, :, :].bitcast(F32), 1.0)

            @block.tensor
            def _(pe):
                pe.wait_ge(table_landed, 48)
                for j in range(NCH):
                    if j >= 4:
                        pe.wait_ge(u_copied, j - 3)
                    nc.tensor.matmul(u_ps[0:NH, j % 4, 0:CH], table[:, :], onehot[:, j * CH:(j + 1) * CH],
                                     start=True, stop=True).then_inc(u_ready, 1)


def attention(nc, dram, images, x_hi, x_lo, wv, v, k_hi1, q_hi2, ident, spread):
    with ExitStack() as ctx:
        def sb(name, shape, dt=F32):
            return ctx.enter_context(nc.sbuf_tensor(name, shape, dt))

        def ps(name):
            return ctx.enter_context(nc.psum_tensor(name, [P, 2, 512], F32))

        def sem(name):
            return ctx.enter_context(nc.semaphore(name))

        STEPS = NH * TILES
        RING = 4
        bias = sb("bias", [TILE, NH, WINDOW])
        w_qk = sb("w_qk", [P, 2, 2, KC, P], F32R)
        probs = sb("probs", [TILE, RING, S])
        q_f = sb("q_f", [P, 2, S])
        k_f = sb("k_f", [P, 2, S])
        k_hilo = sb("k_hilo", [P, 2, S], F32R)
        q_lom = sb("q_lom", [DK + TILES, 2, SPAD], F32R)
        ctx_sb = sb("ctx_sb", [DK + 1, S])
        half_maxima = sb("half_maxima", [TILE, 2, TILES])
        maxima = sb("maxima", [TILE, TILES])
        b_qk = sb("b_qk", [P, 2, PAIRS])
        bv = sb("bv", [TILE, D])
        st = [ps("st0"), ps("st1")]
        s1 = ps("s1")
        ct = ps("ct")

        x_landed = sem("x_landed")
        x_upper_done = sem("x_upper_done")
        x_split = sem("x_split")
        wqk_landed = sem("wqk_landed")
        small_landed = sem("small_landed")
        bias_landed = sem("bias_landed")
        qk_ready = sem("qk_ready")
        qk_staged = sem("qk_staged")
        head_hi = sem("head_hi")
        hi_copied = sem("hi_copied")
        q_lo_done = sem("q_lo_done")
        lo_split = sem("lo_split")
        v_ready = sem("v_ready")
        v_staged = sem("v_staged")
        first_ready = sem("first_ready")
        first_seen = sem("first_seen")
        maxed = sem("maxed")
        max_joined = sem("max_joined")
        turned = sem("turned")
        max_spread = sem("max_spread")
        scores_ready = sem("scores_ready")
        biased = sem("biased")
        exped = sem("exped")
        pv_done = sem("pv_done")
        ctx_copied = sem("ctx_copied")
        ctx_stored = sem("ctx_stored")

        N = None
        FIRST = [[(N, N, N), (N, 0, N), (N, 1, N), (2, N, 3), (N, 4, N), (5, N, 6), (N, 7, N), (N, N, N)],
                 [(N, N, N), (N, N, N), (N, 0, N), (1, N, N), (2, N, 3), (4, N, 5), (6, N, 7), (N, N, N)]]
        FIRST_V = [[], [], [0, 1], [2, 3], [4, 5], [6, 7], [], []]
        TURN_V = 6
        WEIGHED = [[0, 1, 1, 1, 1, 1, 1, 2], [1, 0, 1, 1, 1, 1, 1, 2]]

        def halves(a):
            return a.rearrange("p (t n) -> p t n", t=2)

        def window(h, rows, top):
            stop = top - S
            return halves(bias[0:rows, h, top:(stop if stop >= 0 else None):-1])

        def projected(h):
            return h // 2 + 1 if h % 2 == 0 and h // 2 + 1 < PAIRS else None

        def each_image(eng, image):
            with eng.Fori(0, images - 1) as b:
                image(b, True)
            image(images - 1, False)

        from_one = [x_split, qk_ready, v_ready, lo_split, max_spread, scores_ready, biased, pv_done, ctx_copied,
                    ctx_stored]
        with nc.Block() as block:
            @block.sync
            def _(sp):
                for counted in from_one:
                    sp.sem_inc(counted, 1)

        with nc.Block() as block:
            @block.sync
            def _(sp):
                def load_pair(c):
                    sp.dma_start(w_qk[:, :, :, :, :].rearrange("p i s k n -> p (i s k n)").bitcast(F32),
                                 dram["qk_weights"][c]).then_inc(wqk_landed, 16)

                sp.dma_start(b_qk[:, 0], dram["b_q"]).then_inc(small_landed, 16)
                sp.dma_start(b_qk[:, 1], dram["b_k"]).then_inc(small_landed, 16)
                sp.dma_start(bv[:, :], dram["b_v"].to_broadcast([TILE, D])).then_inc(small_landed, 16)
                load_pair(0)
                for a in range(ROWS):
                    o = (ROWS - 1 - a) * GRID
                    sp.dma_start(bias[a * GRID:(a + 1) * GRID, :, :],
                                 dram["skew"][:, :, o:o + WINDOW].rearrange("h w n -> w h n")).then_inc(bias_landed, 16)

                def image(b, has_next):
                    for c in range(1, PAIRS):
                        sp.wait_ge(qk_ready, b * (2 * PAIRS) + (2 * c + 1))
                        load_pair(c)
                    if has_next:
                        sp.wait_ge(v_ready, b * TILES + (TILES + 1))
                        sp.wait_ge(qk_ready, b * (2 * PAIRS) + (2 * PAIRS + 1))
                        load_pair(0)
                        with sp.Fori(0, KC) as k:
                            sp.dma_start(x_lo[:, bass.ds(k, 1)].rearrange("p a n -> p (a n)").bitcast(F32),
                                         dram["x_t"][bass.ds(k * P, P), bass.ds(b * S + S, S)]).then_inc(x_landed, 16)

                each_image(sp, image)

            @block.gpsimd
            def _(pool):
                def lower_qk(b, h):
                    s, j, r = h % 2, h // 2 % 2, DK * (h % 2)
                    pool.wait_ge(hi_copied, b * NH + (h + 1))
                    nc.gpsimd.tensor_tensor(q_lom[0:DK, s, 0:S], q_f[r:r + DK, j], q_hi2[r:r + DK, s, 0:S].bitcast(F32),
                                            ALU.subtract).then_inc(q_lo_done, 1)
                    pool.wait_ge(q_lo_done, b * NH + (h + 1))
                    nc.gpsimd.tensor_tensor(k_hilo[DK:P, s], k_f[r:r + DK, j], k_hilo[r:r + DK, s].bitcast(F32),
                                            ALU.subtract).then_inc(lo_split, 1)
                    pool.wait_ge(lo_split, b * NH + (h + 2))

                def lower_x(b, k):
                    pool.wait_ge(x_upper_done, b * KC + (k + 1))
                    nc.gpsimd.tensor_tensor(x_lo[:, k], x_lo[:, k].bitcast(F32), x_hi[:, k].bitcast(F32),
                                            ALU.subtract).then_inc(x_split, 1)
                    pool.wait_ge(x_split, b * KC + (k + 2))

                def image(b, has_next):
                    lower_qk(b, 0)
                    for h in range(1, NH):
                        lower_qk(b, h)
                    if has_next:
                        for k in range(KC):
                            lower_x(b, k)

                each_image(pool, image)

            @block.scalar
            def _(act):
                def stage(b, i, c):
                    act.wait_ge(qk_ready, b * (2 * PAIRS) + (2 * c + i + 2))
                    act.wait_ge(lo_split, b * NH + max(2 * c - 1, 1))
                    src = st[0] if c == 0 and i == 1 else s1
                    out = halves(q_f[:, c % 2, S - 1::-1]) if i == 0 else halves(k_f[:, c % 2])
                    nc.scalar.activation(out, src[:, :, 0:HALF], ACT.Identity, bias=b_qk[:, i, c:c + 1],
                                         scale=SCALE if i == 0 else 1.0).then_inc(qk_staged, 1)

                def upper(b, h, part):
                    s, j, r = h % 2, h // 2 % 2, DK * (h % 2)
                    if part == 0:
                        act.wait_ge(qk_staged, b * (2 * PAIRS) + (2 * (h // 2) + 2))
                        act.wait_ge(scores_ready, b * STEPS + (1 + (TILES * (h - 1) if h else 0)))
                        nc.scalar.activation(q_hi2[0:DK, s, 0:S], q_f[r:r + DK, j], ACT.Copy)
                        nc.scalar.activation(k_hilo[0:DK, s], k_f[r:r + DK, j], ACT.Copy).then_inc(head_hi, 1)
                    else:
                        nc.scalar.activation(q_hi2[DK:P, s, 0:S], q_f[r:r + DK, j], ACT.Copy)
                        if r:
                            nc.scalar.activation(k_hilo[DK:P, s], k_f[r:r + DK, j], ACT.Copy)
                        nc.scalar.activation(k_hi1[0:DK, s], k_f[r:r + DK, j], ACT.Copy).then_inc(hi_copied, 1)

                def upper_x(b, k):
                    act.wait_ge(x_landed, b * (KC * 16) + KC * 16)
                    nc.scalar.activation(x_hi[:, k], x_lo[:, k].bitcast(F32), ACT.Copy).then_inc(x_upper_done, 1)

                def exponentials(b, h, t):
                    s = TILES * h + t
                    act.wait_ge(biased, b * STEPS + (s + 2))
                    a = probs[0:tile_rows(t), s % RING]
                    nc.scalar.activation(a, a, ACT.Exp).then_inc(exped, 1)

                def take_context(b, h):
                    act.wait_ge(pv_done, b * STEPS + (TILES * (h + 1) + 1))
                    act.wait_ge(ctx_stored, b * (NH * 32) + (h * 32 + 1))
                    nc.scalar.activation(halves(ctx_sb[:, S - 1::-1]), ct[0:DK + 1, :, 0:HALF], ACT.Copy).then_inc(ctx_copied, 1)

                def store_context(b, h):
                    act.wait_ge(ctx_copied, b * NH + (h + 2))
                    act.dma_start(dram["ctx"][h * DK:(h + 1) * DK, bass.ds(b * S, S)], ctx_sb[0:DK, :]).then_inc(ctx_stored, 16)
                    act.dma_start(dram["sums"][h:h + 1, bass.ds(b * S, S)], ctx_sb[DK:DK + 1, :]).then_inc(ctx_stored, 16)

                act.wait_ge(small_landed, 48)
                nc.scalar.mul(b_qk[:, 0], b_qk[:, 0], SCALE).then_inc(small_landed, 1)
                act.wait_ge(small_landed, 49)

                def image(b, has_next):
                    stage(b, 0, 0)
                    stage(b, 1, 0)
                    upper(b, 0, 0)
                    upper(b, 0, 1)
                    for h in range(NH):
                        if h + 1 < NH:
                            upper(b, h + 1, 0)
                        for t in range(TILES):
                            exponentials(b, h, t)
                            if t < 2 and projected(h):
                                stage(b, t, projected(h))
                            if h and t == (0 if projected(h) else 1):
                                take_context(b, h - 1)
                            if t == 2 and h:
                                store_context(b, h - 1)
                            if t == 2 and h + 1 < NH:
                                upper(b, h + 1, 1)
                            if has_next and h == NH - 2 and 3 <= t < 3 + KC:
                                upper_x(b, t - 3)
                    take_context(b, NH - 1)
                    store_context(b, NH - 1)

                each_image(act, image)
                act.wait_ge(ctx_stored, images * NH * 32 + 1)

            @block.vector
            def _(dve):
                def take_v(b, t):
                    dve.wait_ge(v_ready, b * TILES + (t + 2))
                    m = tile_rows(t)
                    nc.vector.tensor_tensor(v[0:m, t, :, 0:DK], st[(t // 2 + 1) % 2][0:m, t % 2, :].rearrange("p (h n) -> p h n", n=DK),
                                            bv[0:m, :].rearrange("p (h n) -> p h n", n=DK), ALU.add).then_inc(v_staged, 1)

                def first_max(b, h, t):
                    top = (SHIFTS - ROWS + 1 - ROWS * t) * GRID + GRID - 1
                    for n in range(2):
                        dve.wait_ge(first_ready, b * (2 * STEPS) + (2 * (TILES * h + t) + n + 1))
                        dve.sem_inc(first_seen, 1)
                        nc.vector.tensor_tensor_reduce(s1[0:TILE, n, 0:HALF], s1[0:TILE, n, 0:HALF], window(h, TILE, top)[:, n],
                                                       1.0, -3e38, ALU.add, ALU.max, half_maxima[:, n, t:t + 1]).then_inc(maxed, 1)

                def join_max(b, h):
                    dve.wait_ge(maxed, b * (2 * STEPS) + 2 * TILES * (h + 1))
                    nc.vector.tensor_tensor(maxima[:, :], half_maxima[:, 0], half_maxima[:, 1], ALU.max).then_inc(max_joined, 1)

                def spread_max(b, h):
                    dve.wait_ge(turned, b * NH + (h + 1))
                    a = s1[0:TILES, 0:1, 0:TILE].to_broadcast([TILES, TILES, TILE])
                    nc.vector.tensor_tensor(q_lom[DK:DK + TILES, h % 2, :].rearrange("p (a n) -> p a n", a=TILES),
                                            a, spread[:, :, :], ALU.mult).then_inc(max_spread, 1)

                def add_bias(b, h, t):
                    s, m = TILES * h + t, tile_rows(t)
                    dve.wait_ge(scores_ready, b * STEPS + (s + 2))
                    if s >= RING:
                        dve.wait_ge(pv_done, b * STEPS + (s - RING + 2))
                    top = ROWS * (TILES - 1 - t) * GRID + S - 1
                    nc.vector.tensor_tensor(halves(probs[0:m, s % RING, :]), st[s % 2][0:m, :, 0:HALF], window(h, m, top),
                                            ALU.add).then_inc(biased, 1)

                dve.wait_ge(small_landed, 48)
                dve.wait_ge(bias_landed, 16 * ROWS)

                def image(b, has_next):
                    dve.wait_ge(pv_done, b * STEPS + 1)
                    for t in range(TILES):
                        for i in FIRST_V[t]:
                            first_max(b, 0, i)
                        if t == TURN_V:
                            spread_max(b, 0)
                        take_v(b, t)
                        if t == TURN_V - 1:
                            join_max(b, 0)
                    for h in range(NH):
                        for t in range(TILES):
                            before, after, between = FIRST[projected(h) is not None][t] if h + 1 < NH else (N, N, N)
                            if before is not N:
                                first_max(b, h + 1, before)
                            add_bias(b, h, t)
                            if t == TILES - 1 and h + 1 < NH:
                                spread_max(b, h + 1)
                            for i in (after, between):
                                if i is not N:
                                    first_max(b, h + 1, i)
                            if t == TILES - 2 and h + 1 < NH:
                                join_max(b, h + 1)

                each_image(dve, image)

            @block.tensor
            def _(pe):
                def project(b, i, c):
                    out = s1
                    if i == 0:
                        pe.wait_ge(wqk_landed, (b * PAIRS + (c + 1)) * 16)
                        if c == 0:
                            pe.wait_ge(x_split, b * KC + 1)
                        pe.wait_ge(max_spread, b * NH + max(2 * c, 1))
                    elif c == 0:
                        out = st[0]
                        pe.wait_ge(biased, b * STEPS + 1)
                    else:
                        pe.wait_ge(qk_staged, b * (2 * PAIRS) + (2 * c + 1))
                    for k in range(KC):
                        for w, xs in ((0, x_hi), (0, x_lo), (1, x_hi)):
                            for n in range(2):
                                mm = nc.tensor.matmul(out[:, n, 0:HALF], w_qk[:, i, w, k, :],
                                                      xs[:, k, n * HALF:(n + 1) * HALF],
                                                      start=(k == 0 and w == 0 and xs is x_hi),
                                                      stop=(k == KC - 1 and w == 1))
                    mm.then_inc(qk_ready, 1)

                def project_v(b, t, between):
                    m = tile_rows(t)
                    if t == 2:
                        pe.wait_ge(qk_staged, b * (2 * PAIRS) + 2)
                    if t < 4:
                        pe.wait_ge(biased, b * STEPS + 1)
                    else:
                        pe.wait_ge(v_staged, b * TILES + (t - 3))
                    for k in range(KC):
                        for xs, w in ((x_hi, 0), (x_hi, 1), (x_lo, 0)):
                            mm = nc.tensor.matmul(st[(t // 2 + 1) % 2][0:m, t % 2, :], xs[:, k, t * TILE:t * TILE + m], wv[:, w, k],
                                                  start=(k == 0 and xs is x_hi and w == 0),
                                                  stop=(k == KC - 1 and xs is x_lo))
                        if k == KC // 2 - 1 and between:
                            first_scores(b, 0, between[0])
                    mm.then_inc(v_ready, 1)
                    for i in between[1:]:
                        first_scores(b, 0, i)

                def first_scores(b, h, t):
                    s = h % 2
                    if t == 0:
                        pe.wait_ge(head_hi, b * NH + (h + 1))
                        pe.wait_ge(qk_staged, b * (2 * PAIRS) + min(2 * ((h + 1) // 2 + 1), 2 * PAIRS))
                        if h:
                            pe.wait_ge(max_spread, b * NH + (h + 1))
                    for n in range(2):
                        if t:
                            pe.wait_ge(maxed, b * (2 * STEPS) + (2 * (TILES * h + t) + n - 1))
                        nc.tensor.matmul(s1[0:TILE, n, 0:HALF], q_hi2[0:DK, s, t * TILE:(t + 1) * TILE],
                                              k_hilo[0:DK, s, n * HALF:(n + 1) * HALF], start=True, stop=True)\
                            .then_inc(first_ready, 1)

                def turn_max(b, h):
                    pe.wait_ge(max_joined, b * NH + (h + 1))
                    nc.tensor.matmul(s1[0:TILES, 0, 0:TILE], maxima[:, :], ident[:, :], start=True, stop=True)\
                      .then_inc(turned, 1)

                def scores(b, h, t):
                    s, m, i = h % 2, tile_rows(t), TILES * h + t
                    if t == 0:
                        pe.wait_ge(lo_split, b * NH + (h + 2))
                        pe.wait_ge(max_spread, b * NH + (h + 2))
                    if i < 2:
                        pe.wait_ge(v_staged, b * TILES + TILES)
                    else:
                        pe.wait_ge(biased, b * STEPS + i)
                    for n in range(2):
                        q = slice(n * HALF, (n + 1) * HALF)
                        nc.tensor.matmul(st[i % 2][0:m, n, 0:HALF], k_hilo[:, s, t * TILE:t * TILE + m], q_hi2[:, s, q],
                                         start=True, stop=False)
                    for n in range(2):
                        q = slice(n * HALF, (n + 1) * HALF)
                        mm = nc.tensor.matmul(st[i % 2][0:m, n, 0:HALF], k_hi1[:, s, t * TILE:t * TILE + m], q_lom[:, s, q],
                                              start=False, stop=True)
                    mm.then_inc(scores_ready, 1)

                def weigh_values(b, h, t, h_next=None, between=None):
                    m, i = tile_rows(t), TILES * h + t
                    pe.wait_ge(exped, b * STEPS + (i + 1))
                    if t == 0:
                        pe.wait_ge(ctx_copied, b * NH + (h + 1))
                    for n in range(2):
                        mm = nc.tensor.matmul(ct[0:DK + 1, n, 0:HALF], v[0:m, t, h], probs[0:m, i % RING, n * HALF:(n + 1) * HALF],
                                              start=(t == 0), stop=(t == TILES - 1))
                        if n == 0 and between is not N:
                            first_scores(b, h_next, between)
                    mm.then_inc(pv_done, 1)

                def image(b, has_next):
                    project(b, 1, 0)
                    for t in range(TILES):
                        if t == TURN_V:
                            turn_max(b, 0)
                        project_v(b, t, FIRST_V[t])
                    late = []
                    for h in range(NH):
                        for t in range(TILES):
                            before, after, between = FIRST[projected(h) is not None][t] if h + 1 < NH else (N, N, N)
                            if before is not N:
                                first_scores(b, h + 1, before)
                            scores(b, h, t)
                            if t == TILES - 1 and h + 1 < NH:
                                turn_max(b, h + 1)
                            late.append((h, t))
                            if t == 0 and projected(h):
                                project(b, 0, projected(h))
                            if after is not N:
                                first_scores(b, h + 1, after)
                            for u in range(WEIGHED[projected(h) is not None][t] if late[1:] else 0):
                                weigh_values(b, *late.pop(0), h + 1, between if not u else N)
                            if t == 1 and projected(h):
                                project(b, 1, projected(h))
                    if has_next:
                        project(b + 1, 0, 0)
                    for at in late:
                        weigh_values(b, *at)

                project(0, 0, 0)
                each_image(pe, image)


TOKENS = IMAGES * S
SUB = 120
SUBS = 3
TT = SUB * SUBS
NT = TOKENS // TT
NEWTON = 3
RSQRT_MAGIC = 0x5F3759DF


def feed_forward(nc, dram):
    with ExitStack() as ctx:
        def sb(name, shape, dt=F32):
            return ctx.enter_context(nc.sbuf_tensor(name, shape, dt))

        def ps(name, shape):
            return ctx.enter_context(nc.psum_tensor(name, shape, F32))

        def sem(name):
            return ctx.enter_context(nc.semaphore(name))

        wo = [sb(f"wo_{p}", [P, KC, D], F32R) for p in ("hi", "lo")]
        w1 = [sb(f"w1_{p}", [P, KC, FF], F32R) for p in ("hi", "lo")]
        w2 = [sb(f"w2_{p}", [P, FC, D], F32R) for p in ("hi", "lo")]
        bo_row, g1_row, be1_row, g2_row, be2_row = (sb(n, [SUB, D]) for n in ("bo_row", "g1_row", "be1_row", "g2_row", "be2_row"))
        b1_col = sb("b1_col", [P, FC])
        g1_col = sb("g1_col", [P, KC])
        be1_col = sb("be1_col", [P, KC])
        ident = sb("ident2", [SUB, SUB])
        y_ps = ps("y_ps", [P, SUBS, 512])
        h_ps = ps("h_ps", [P, 2, 512])
        z_ps = ps("z_ps", [P, SUBS, 512])

        weights = [("w_o", wo, 0, KC), ("w1", w1, 0, KC // 2), ("w1", w1, KC // 2, KC)]
        weights += [("w2", w2, f, f + KC) for f in range(0, FC, KC)]

        weights_landed = [sem(f"weights_landed{n}") for n in range(len(weights))]
        weights_hi = sem("weights_hi")
        weights_lo = sem("weights_lo")
        rows_landed = sem("rows_landed")
        rows_added = sem("rows_added")
        sums_landed = sem("sums_landed")
        inverted = sem("inverted")
        inverse_stored = sem("inverse_stored")
        ident_set = sem("ident_set")

        b2_row = sb("b2_row", [SUB, D])
        sums = sb("sums_sb", [P, NH * TOKENS // P])
        c_raw = sb("c_raw", [P, 2, TT])
        c_inv = sb("c_inv", [P, 2, TT])
        res = sb("res", [SUB, 2, SUBS, D])
        parts_t = [[sb(f"parts_{p}_{e}", [P, KC, TT], F32R) for p in ("hi", "lo")] for e in range(2)]
        g = sb("g", [P, 2, TT])
        h_t = [sb(f"h_{p}", [P, 2, TT], F32R) for p in ("hi", "lo")]
        stats = sb("stats", [SUB, 6])
        mean_var = sb("mean_var", [SUB, SUBS, 2])
        var = sb("var", [SUB, SUBS])
        root = sb("root", [SUB, SUBS])
        step = sb("step", [SUB, SUBS])

        ctx_landed = [sem("ctx_landed0"), sem("ctx_landed1")]
        sp_passed = sem("sp_passed")
        divided = sem("divided")
        ctx_hi = sem("ctx_hi")
        ctx_split = sem("ctx_split")
        x_landed = [sem("x_landed_even"), sem("x_landed_odd")]
        x_biased = sem("x_biased")
        z_ready = sem("z_ready")
        z_taken = sem("z_taken")
        ln_step = sem("ln_step")
        ln_passed = sem("ln_passed")
        normed1 = sem("normed1")
        normed2 = sem("normed2")
        turned = sem("turned2")
        turn_staged = sem("turn_staged")
        a_hi = sem("a_hi")
        a_split = sem("a_split")
        h_ready = sem("h_ready")
        g_done = sem("g_done")
        h_hi = sem("h_hi")
        h_split = sem("h_split")
        y_step = sem("y_step")
        y_taken = sem("y_taken")
        scaled = sem("scaled")
        residual_ready = sem("residual_ready")
        out_ready = sem("out_ready")
        last_ready = sem("last_ready")
        out_stored = [sem("out_stored_even"), sem("out_stored_odd")]
        LN_OPS = SUBS * 2 + 3 + 3 * NEWTON
        CONTEXT_AT, OUT_AT, NORM_AT, TURN_AT = 2, 6, 8, 13
        TURNED = [[]] * TURN_AT + [[0, 1, 2], [3]] + [[]] * (FC - TURN_AT - 2)
        TAKEN = [[]] * TURN_AT + [[0, 1], [2, 3]] + [[]] * (FC - TURN_AT - 2)

        def tiles(eng, front, body, tail):
            front(0, 0, 0)
            body(0, 0, 0, False, True)
            with eng.Fori(0, (NT - 2) // 2) as u:
                body(u * 2 + 1, u, 1, True, True)
                body(u * 2 + 2, u + 1, 0, True, True)
            body(NT - 1, (NT - 1) // 2, 1, True, False)
            tail(NT - 1, 1)

        def scale_and_shift(eng, ops, n, e, g_row, b_row, done):
            for s in range(SUBS):
                ops.tensor_tensor(res[:, e, s], res[:, e, s], g_row[:, :], ALU.mult).then_inc(scaled, 1)
            eng.wait_ge(scaled, n * SUBS + SUBS)
            for s in range(SUBS):
                i = ops.tensor_tensor(res[:, e, s], res[:, e, s], b_row[:, :], ALU.add)
            i.then_inc(done, 1)

        def nothing(*_):
            return None

        with nc.Block() as block:
            @block.sync
            def _(sp):
                def load_context(t, c):
                    if c == 0:
                        sp.wait_ge(a_split, t * KC)
                    sp.wait_ge(ctx_split, t * KC + (c - 1 if c >= 2 else 0))
                    sp.sem_inc(sp_passed, 1)
                    sp.dma_start(c_raw[:, c % 2], dram["ctx"][c * P:(c + 1) * P, bass.ds(t * TT, TT)])\
                      .then_inc(ctx_landed[c % 2], 16)
                    for i in range(2):
                        sp.dma_start(c_inv[i * DK:(i + 1) * DK, c % 2],
                                     dram["inverse"][2 * c + i:2 * c + i + 1, bass.ds(t * TT, TT)].to_broadcast([DK, TT]))\
                          .then_inc(ctx_landed[c % 2], 16)

                def load_x(t, u, e):
                    sp.wait_ge(out_stored[e], u * 16)
                    sp.dma_start(res[:, e], dram["x"][bass.ds(t * TT, TT), :].rearrange("(s p) n -> p s n", p=SUB))\
                      .then_inc(x_landed[e], 16)

                def load_weights(n):
                    name, to, begin, end = weights[n]
                    with sp.Fori(begin, end) as k:
                        sp.dma_start(to[1][:, bass.ds(k, 1)].rearrange("p a n -> p (a n)").bitcast(F32),
                                     dram[name][bass.ds(k * P, P), :]).then_inc(weights_landed[n], 16)

                def front(t, u, e):
                    sp.dma_start(sums[:, :], dram["sums"].rearrange("h (a n) -> (h a) n", a=P // NH)).then_inc(sums_landed, 16)
                    load_weights(0)
                    for row, name in ((bo_row, "b_o"), (g1_row, "ln1_g"), (be1_row, "ln1_b"), (g2_row, "ln2_g"),
                                      (be2_row, "ln2_b"), (b2_row, "b2")):
                        sp.dma_start(row[:, :], dram[name].to_broadcast([SUB, D])).then_inc(rows_landed, 16)
                    for col, name in ((b1_col, "b1"), (g1_col, "ln1_g_col"), (be1_col, "ln1_b_col")):
                        sp.dma_start(col[:, :], dram[name]).then_inc(rows_landed, 16)
                    load_x(t, u, e)
                    sp.wait_ge(inverted, 1)
                    sp.dma_start(dram["inverse"].rearrange("h (a n) -> (h a) n", a=P // NH), sums[:, :])\
                      .then_inc(inverse_stored, 16)
                    load_weights(1)
                    sp.wait_ge(inverse_stored, 16)
                    load_context(t, 0)
                    load_context(t, 1)
                    load_weights(2)
                    load_context(t, 2)
                    load_context(t, 3)
                    for n in range(3, len(weights)):
                        load_weights(n)

                def store(t, e, ready, n):
                    sp.wait_ge(ready, n)
                    sp.dma_start(dram["out"][bass.ds(t * TT, TT), :].rearrange("(s p) n -> p s n", p=SUB), res[:, e])\
                      .then_inc(out_stored[e], 16)

                def body(t, u, e, has_prev, has_next):
                    if has_next:
                        for c in range(KC):
                            load_context(t + 1, c)
                    if has_prev:
                        store(t - 1, 1 - e, out_ready, t)
                    if has_next:
                        load_x(t + 1, u + e, 1 - e)

                def tail(t, e):
                    store(t, e, last_ready, 1)

                tiles(sp, front, body, tail)
                sp.wait_ge(out_stored[0], NT // 2 * 16)
                sp.wait_ge(out_stored[1], NT // 2 * 16)

            @block.gpsimd
            def _(pool):
                def divide_context(t, e):
                    for c in range(KC):
                        pool.wait_ge(ctx_landed[c % 2], (t * 2 + (c // 2 + 1)) * 48)
                        nc.gpsimd.tensor_tensor(c_raw[:, c % 2], c_raw[:, c % 2], c_inv[:, c % 2], ALU.mult).then_inc(divided, 1)
                        pool.wait_ge(ctx_hi, t * KC + (c + 1))
                        nc.gpsimd.tensor_tensor(parts_t[e][1][:, c], c_raw[:, c % 2], parts_t[e][0][:, c].bitcast(F32),
                                                ALU.subtract).then_inc(ctx_split, 1)

                def bias_x(u, e):
                    pool.wait_ge(x_landed[e], (u + 1) * 16)
                    for s in range(SUBS):
                        nc.gpsimd.tensor_tensor(res[:, e, s], res[:, e, s], bo_row[:, :], ALU.add).then_inc(x_biased, 1)

                def body(t, u, e, has_prev, has_next):
                    if has_next:
                        divide_context(t + 1, 1 - e)
                    if has_prev:
                        pool.wait_ge(normed2, t * SUBS)
                        scale_and_shift(pool, nc.gpsimd, t * 2, 1 - e, g2_row, be2_row, out_ready)
                    if has_next:
                        bias_x(u + e, 1 - e)
                        pool.wait_ge(turned, t * KC + 2 * KC)
                        scale_and_shift(pool, nc.gpsimd, t * 2 + 1, 1 - e, g1_row, be1_row, residual_ready)

                def first(t, u, e):
                    nc.gpsimd.memset(ident[:, :], 0.0).then_inc(ident_set, 1)
                    pool.wait_ge(ident_set, 1)
                    nc.gpsimd.affine_select(out=ident[:, :], in_=ident[:, :], compare_op=ALU.not_equal, fill=1.0,
                                            base=0, pattern=[[-1, SUB]], channel_multiplier=1).then_inc(ident_set, 1)
                    pool.wait_ge(rows_landed, 16 * 9)
                    nc.gpsimd.tensor_tensor(be1_row[:, :], be1_row[:, :], b2_row[:, :], ALU.add).then_inc(rows_added, 1)
                    divide_context(t, e)
                    bias_x(u, e)
                    pool.wait_ge(rows_added, 1)
                    pool.wait_ge(turned, KC)
                    scale_and_shift(pool, nc.gpsimd, 0, e, g1_row, be1_row, residual_ready)

                tiles(pool, first, body, nothing)

            @block.scalar
            def _(act):
                def weights_upper(n):
                    _, to, begin, end = weights[n]
                    act.wait_ge(weights_landed[n], (end - begin) * 16)
                    nc.scalar.activation(to[0][:, begin:end], to[1][:, begin:end].bitcast(F32), ACT.Copy).then_inc(weights_hi, 1)

                def context_upper(t, e, c):
                    act.wait_ge(divided, t * KC + (c + 1))
                    nc.scalar.activation(parts_t[e][0][:, c], c_raw[:, c % 2], ACT.Copy).then_inc(ctx_hi, 1)

                def take_turned(t, e, c):
                    act.wait_ge(turned, t * KC + (c + 1))
                    if c < 2:
                        act.wait_ge(ctx_split, t * KC + KC)
                    else:
                        act.wait_ge(a_split, t * KC + (c - 1))
                    nc.scalar.activation(c_raw[:, c % 2], z_ps[:, c % SUBS, 0:TT], ACT.Identity, bias=be1_col[:, c:c + 1],
                                         scale=g1_col[:, c:c + 1]).then_inc(turn_staged, 1)
                    act.wait_ge(turn_staged, t * KC + (c + 1))
                    nc.scalar.activation(parts_t[e][0][:, c], c_raw[:, c % 2], ACT.Copy).then_inc(a_hi, 1)

                def gelu(t, f):
                    act.wait_ge(h_ready, t * FC + (f + 1))
                    act.wait_ge(h_split, t * FC + (f - 1 if f >= 2 else 0))
                    nc.scalar.activation(g[:, f % 2], h_ps[:, f % 2, 0:TT], ACT.Gelu, bias=b1_col[:, f:f + 1])\
                      .then_inc(g_done, 1)
                    act.wait_ge(y_step, t * FC + (f - 1 if f >= 2 else 0))
                    act.wait_ge(g_done, t * FC + (f + 1))
                    nc.scalar.activation(h_t[0][:, f % 2], g[:, f % 2], ACT.Copy).then_inc(h_hi, 1)

                def front(t, u, e):
                    for n in range(2):
                        weights_upper(n)
                    context_upper(t, e, 0)
                    context_upper(t, e, 1)
                    weights_upper(2)
                    context_upper(t, e, 2)
                    context_upper(t, e, 3)
                    for n in range(3, len(weights)):
                        weights_upper(n)
                    act.wait_ge(rows_landed, 16 * 9)
                    for c in range(KC):
                        take_turned(t, e, c)

                def body(t, u, e, has_prev, has_next):
                    for f in range(FC):
                        gelu(t, f)
                        if CONTEXT_AT <= f < CONTEXT_AT + KC and has_next:
                            context_upper(t + 1, 1 - e, f - CONTEXT_AT)
                        for c in TAKEN[f] if has_next else ():
                            take_turned(t + 1, 1 - e, c)

                tiles(act, front, body, nothing)

            @block.vector
            def _(dve):
                def then(i, q, n):
                    i.then_inc(ln_step, 1)
                    dve.wait_ge(ln_step, q * LN_OPS + n)

                def moments(q, e, s):
                    then(nc.vector.bn_stats(stats[:, :], res[:, e, s]), q, 2 * s + 1)
                    dve.sem_inc(ln_passed, 1)
                    then(nc.vector.bn_aggr(mean_var[:, s, :], stats[:, :]), q, 2 * s + 2)

                def inverse_roots(q):
                    n = 2 * SUBS
                    bits = root[:, :].bitcast(I32)
                    then(nc.vector.tensor_scalar(var[:, :], mean_var[:, :, 1], LN_EPS, None, ALU.add), q, n + 1)
                    then(nc.vector.tensor_scalar(bits, var[:, :].bitcast(I32), 1, None, ALU.logical_shift_right), q, n + 2)
                    then(nc.vector.tensor_scalar(bits, bits, -1.0, float(RSQRT_MAGIC), ALU.mult, ALU.add), q, n + 3)
                    n += 3
                    for _ in range(NEWTON):
                        then(nc.vector.tensor_tensor(step[:, :], root[:, :], root[:, :], ALU.mult), q, n + 1)
                        then(nc.vector.scalar_tensor_tensor(out=step[:, :], in0=step[:, :], scalar=-0.5, in1=var[:, :],
                                                            op0=ALU.mult, op1=ALU.mult), q, n + 2)
                        then(nc.vector.scalar_tensor_tensor(out=root[:, :], in0=step[:, :], scalar=1.5, in1=root[:, :],
                                                            op0=ALU.add, op1=ALU.mult), q, n + 3)
                        n += 3

                def normalise(e, done):
                    for s in range(SUBS):
                        nc.vector.tensor_scalar(res[:, e, s], res[:, e, s], mean_var[:, s, 0:1], root[:, s:s + 1],
                                                ALU.subtract, ALU.mult).then_inc(done, 1)

                def take_z(t, e, s):
                    dve.wait_ge(x_biased, t * SUBS + (s + 1))
                    dve.wait_ge(z_ready, t * SUBS + (s + 1))
                    nc.vector.tensor_tensor(res[:, e, s], z_ps[0:SUB, s, :], res[:, e, s], ALU.add).then_inc(z_taken, 1)
                    dve.wait_ge(z_taken, t * SUBS + (s + 1))

                def a_lower(t, e, c):
                    dve.wait_ge(a_hi, t * KC + (c + 1))
                    nc.vector.tensor_tensor(parts_t[e][1][:, c], c_raw[:, c % 2], parts_t[e][0][:, c].bitcast(F32),
                                            ALU.subtract).then_inc(a_split, 1)

                def h_lower(t, f):
                    dve.wait_ge(h_hi, t * FC + (f + 1))
                    nc.vector.tensor_tensor(h_t[1][:, f % 2], g[:, f % 2], h_t[0][:, f % 2].bitcast(F32),
                                            ALU.subtract).then_inc(h_split, 1)

                def take_y(t, e):
                    dve.wait_ge(residual_ready, t + 1)
                    dve.wait_ge(y_step, t * FC + FC)
                    for s in range(SUBS):
                        nc.vector.tensor_tensor(res[:, e, s], y_ps[0:SUB, s, :], res[:, e, s], ALU.add).then_inc(y_taken, 1)

                def weights_lower(n):
                    dve.wait_ge(weights_hi, n + 1)
                    _, to, begin, end = weights[n]
                    nc.vector.tensor_tensor(to[1][:, begin:end], to[1][:, begin:end].bitcast(F32),
                                            to[0][:, begin:end].bitcast(F32), ALU.subtract).then_inc(weights_lo, 1)

                def front(t, u, e):
                    dve.wait_ge(sums_landed, 16)
                    nc.vector.reciprocal(sums[:, :], sums[:, :]).then_inc(inverted, 1)
                    for n in range(3):
                        weights_lower(n)
                    for s in range(SUBS):
                        take_z(0, 0, s)
                        moments(0, 0, s)
                    inverse_roots(0)
                    normalise(0, normed1)
                    for n in range(3, 4):
                        weights_lower(n)
                    for c in range(KC):
                        a_lower(0, 0, c)

                def body(t, u, e, has_prev, has_next):
                    for f in range(FC):
                        h_lower(t, f)
                        if not has_prev and f in (1, 3, 5):
                            weights_lower(4 + f // 2)
                        if has_prev:
                            if f == 0:
                                dve.wait_ge(y_taken, t * SUBS)
                            if f < SUBS:
                                moments(t * 2, 1 - e, f)
                            if f == SUBS:
                                inverse_roots(t * 2)
                                normalise(1 - e, normed2)
                        if has_next:
                            if NORM_AT <= f < NORM_AT + SUBS:
                                take_z(t + 1, 1 - e, f - NORM_AT)
                                moments(t * 2 + 1, 1 - e, f - NORM_AT)
                            if f == NORM_AT + SUBS:
                                inverse_roots(t * 2 + 1)
                                normalise(1 - e, normed1)
                            for c in TAKEN[f]:
                                a_lower(t + 1, 1 - e, c)
                    take_y(t, e)

                def tail(t, e):
                    dve.wait_ge(y_taken, NT * SUBS)
                    for s in range(SUBS):
                        moments(NT * 2 - 1, e, s)
                    inverse_roots(NT * 2 - 1)
                    normalise(e, normed2)
                    dve.wait_ge(scaled, (NT * 2 - 1) * SUBS)
                    dve.wait_ge(normed2, NT * SUBS)
                    scale_and_shift(dve, nc.vector, NT * 2 - 1, e, g2_row, be2_row, last_ready)

                tiles(dve, front, body, tail)

            @block.tensor
            def _(pe):
                PASSES = ((0, 0), (0, 1), (1, 0))

                def project_out(t, e, s):
                    if s == 0:
                        pe.wait_ge(ctx_split, t * KC + KC)
                        pe.wait_ge(turn_staged, t * KC)
                    for k in range(KC):
                        for x, w in PASSES:
                            mm = nc.tensor.matmul(z_ps[0:SUB, s, :], parts_t[e][x][:, k, s * SUB:(s + 1) * SUB], wo[w][:, k, :],
                                                  start=(k + x + w == 0), stop=(k == KC - 1 and x == 1))
                    mm.then_inc(z_ready, 1)

                def turn(t, e, c):
                    if c == 0:
                        pe.wait_ge(normed1, t * SUBS + SUBS)
                    if c >= SUBS:
                        pe.wait_ge(turn_staged, t * KC + (c - SUBS + 1))
                    for s in range(SUBS):
                        mm = nc.tensor.transpose(z_ps[:, c % SUBS, s * SUB:(s + 1) * SUB], res[:, e, s, c * P:(c + 1) * P],
                                                 ident[:, :])
                    mm.then_inc(turned, 1)

                def widen(t, e, f):
                    if f == 0:
                        pe.wait_ge(a_split, t * KC + KC)
                    pe.wait_ge(g_done, t * FC + (f - 1 if f >= 2 else 0))
                    for k in range(KC):
                        for x, w in ((0, 0), (1, 0), (0, 1)):
                            mm = nc.tensor.matmul(h_ps[:, f % 2, 0:TT], w1[w][:, k, f * P:(f + 1) * P], parts_t[e][x][:, k, :],
                                                  start=(k + x + w == 0), stop=(k == KC - 1 and w == 1))
                    mm.then_inc(h_ready, 1)

                def narrow(t, f, first_tile):
                    pe.wait_ge(h_split, t * FC + (f + 1))
                    if first_tile and f % KC == 0:
                        pe.wait_ge(weights_lo, 4 + f // KC)
                    if f == 0:
                        pe.wait_ge(y_taken, t * SUBS)
                    for s in range(SUBS):
                        for x, w in PASSES:
                            mm = nc.tensor.matmul(y_ps[0:SUB, s, :], h_t[x][:, f % 2, s * SUB:(s + 1) * SUB], w2[w][:, f, :],
                                                  start=(f + x + w == 0), stop=(f == FC - 1 and x == 1))
                    mm.then_inc(y_step, 1)

                def front(t, u, e):
                    pe.wait_ge(weights_lo, 1)
                    for s in range(SUBS):
                        project_out(0, 0, s)
                    pe.wait_ge(ident_set, 2)
                    for c in range(KC):
                        turn(0, 0, c)

                def body(t, u, e, has_prev, has_next):
                    for f in range(FC):
                        if not has_prev and f == 0:
                            pe.wait_ge(weights_lo, 3)
                        widen(t, e, f)
                        for c in TURNED[f] if has_next else ():
                            turn(t + 1, 1 - e, c)
                        if f:
                            narrow(t, f - 1, not has_prev)
                        if OUT_AT <= f < OUT_AT + SUBS and has_next:
                            project_out(t + 1, 1 - e, f - OUT_AT)
                    narrow(t, FC - 1, not has_prev)

                tiles(pe, front, body, nothing)


def build(nc, dram, images=IMAGES):
    with ExitStack() as ctx:
        def sb(name, shape, dt=F32):
            return ctx.enter_context(nc.sbuf_tensor(name, shape, dt))

        kept = {
            "x_hi": sb("x_hi", [P, KC, S], F32R),
            "x_lo": sb("x_lo", [P, KC, S], F32R),
            "wv": sb("wv", [P, 2, KC, D], F32R),
            "v": sb("v", [TILE, TILES, NH, DK + 1]),
            "k_hi1": sb("k_hi1", [DK + TILES, 2, S], F32R),
            "q_hi2": sb("q_hi2", [P, 2, SPAD], F32R),
            "ident": sb("ident", [TILE, TILE]),
            "spread": sb("spread", [TILES, TILES, TILE]),
        }
        prepare(nc, dram, **kept)
        attention(nc, dram, images, **kept)
    feed_forward(nc, dram)


def displacement_onehot():
    import numpy as np

    r, c = np.indices((UROWS, UCOLS))
    dh = (GRID + 1 - r).astype(np.float64)
    dw = (GRID - 1 - c).astype(np.float64)
    dist = np.minimum(np.sqrt(dh ** 2 + dw ** 2).astype(np.int64), DISTS - 1)
    direction = ((np.arctan2(dh, dw) + np.pi) / (2.0 * np.pi) * DIRS).astype(np.int64) % DIRS
    direction = np.where((dh == 0) & (dw == 0), 0, direction)
    out = np.zeros((DISTS + DIRS, r.size), np.float32)
    out[dist.ravel(), np.arange(r.size)] = 1.0
    out[DISTS + direction.ravel(), np.arange(r.size)] = 1.0
    return out


def kernel(**inputs):
    import numpy as np
    import concourse.bacc as bacc
    from concourse.bass_utils import run_bass_kernel_spmd

    def given(name):
        return np.ascontiguousarray(inputs[name if name == "x" else "L0_conv_" + name])

    def columns(name):
        return np.ascontiguousarray(given(name).reshape(-1, P).T)

    x = given("x").reshape(TOKENS, D)
    arrays = {"x": x, "x_t": np.ascontiguousarray(x.T), "displacement_onehot": displacement_onehot()}
    for name in ("dist_bias", "dir_bias", "w_q", "w_k", "w_v", "w_o", "w1", "w2"):
        arrays[name] = given(name)
    for name in ("b_q", "b_k", "b1"):
        arrays[name] = columns(name)
    for name in ("b_v", "b_o", "b2", "ln1_g", "ln1_b", "ln2_g", "ln2_b"):
        arrays[name] = given(name).reshape(1, D)
    for name in ("ln1_g", "ln1_b"):
        arrays[name + "_col"] = columns(name)

    nc = bacc.Bacc("TRN2", target_bir_lowering=False, num_devices=1)
    dram = {name: nc.dram_tensor(name, a.shape, mybir.dt.from_np(a.dtype), kind="ExternalInput").ap()
            for name, a in arrays.items()}
    for name, shape in (("skew", (NH, GRID, UROWS * GRID)), ("qk_weights", (PAIRS, P, 4 * KC * P)),
                        ("ctx", (D, TOKENS)), ("sums", (NH, TOKENS)), ("inverse", (NH, TOKENS))):
        dram[name] = nc.dram_tensor(name, shape, F32, kind="Internal").ap()
    dram["out"] = nc.dram_tensor("out", (TOKENS, D), F32, kind="ExternalOutput").ap()
    build(nc, dram)
    got = run_bass_kernel_spmd(nc, [arrays], core_ids=[0])
    return got.results[0]["out"].reshape(IMAGES, GRID, GRID, D)
```
